# Optimizing a Trainium2 kernel written in Bass

```python
import numpy as np
import jax
import jax.numpy as jnp

def _softmax(x, axis=-1):
    return jax.nn.softmax(x, axis=axis)

def _gelu(x):
    return jax.nn.gelu(x, approximate=True)

def _silu(x):
    return jax.nn.silu(x)

def _sigmoid(x):
    return jax.nn.sigmoid(x)

def _layernorm(x, axis=-1, eps=1e-05):
    m = jnp.mean(x, axis=axis, keepdims=True)
    v = jnp.var(x, axis=axis, keepdims=True)
    return (x - m) / jnp.sqrt(v + eps)

def _scatter_add(tgt, idx, src, axis=0):
    return tgt.at[idx].add(src)

def _segment_sum(src, seg, n):
    return jax.ops.segment_sum(src, seg, n)
kernel_name = 'mk_flamingo_gated_d1_seqx_r2_a7fab2'

def setup_inputs(seed: int=0):
    np.random.seed(seed)
    _w = jnp.asarray

    def _rec_inputs():
        import jax
        import jax.numpy as jnp
        _rk = jax.random.key(seed)
        x = 7.22e-05 + 1 * jax.random.normal(jax.random.fold_in(_rk, 1), (2, 2048, 512), jnp.float32)
        _lenS = 2048 - jax.random.randint(jax.random.fold_in(_rk, 7), (2,), 0, max(1, 2048 // 4) + 1, jnp.int32)
        _lenS2 = 128 - jax.random.randint(jax.random.fold_in(_rk, 8), (2,), 0, max(1, 128 // 4) + 1, jnp.int32)
        _ctx_1024P = jax.random.normal(jax.random.fold_in(_rk, 11), (2, 16, 512), jnp.float32)
        _ctx_1024c = jax.random.dirichlet(jax.random.fold_in(_rk, 511), 0.3 * jnp.ones((16,), jnp.float32), (2, 128))
        _ctx_1024t = jnp.einsum('bsk,bkd->bsd', _ctx_1024c, _ctx_1024P)
        _ctx_1024t = _ctx_1024t * jax.lax.rsqrt(jnp.mean(jnp.square(_ctx_1024t)) + 1e-12) * 0.953939
        ctx_1024 = 4.13588e-05 + 0.999923 * (_ctx_1024t + 0.3 * jax.random.normal(jax.random.fold_in(_rk, 611), (2, 128, 512), jnp.float32))
        _g = jax.random.normal(jax.random.fold_in(_rk, 9001), (2, 1), jnp.float32)
        _g = jnp.sign(_g) * jnp.maximum(jnp.abs(_g), 1.0) + (_g == 0) * 1.0
        g_xattn = _g[0]
        g_ffn = _g[1]
        return (x, ctx_1024, g_xattn, g_ffn)
    x, ctx_1024, g_xattn, g_ffn = _rec_inputs()

    def _L0_xattn_setup():
        import jax, jax.numpy as jnp
        import numpy as np
        HEAD_NUM = 16
        D_MODEL = 512
        D_K = D_MODEL // HEAD_NUM
        key = jax.random.key(seed)
        ks = jax.random.split(key, 11)
        B, S = (4, 1024)

        def xavier(k, shape):
            fan_in, fan_out = (shape[1], shape[0])
            lim = np.sqrt(6.0 / (fan_in + fan_out))
            return jax.random.uniform(k, shape, jnp.float32, -lim, lim)
        return {'query': jax.random.normal(ks[0], (B, S, D_MODEL), jnp.float32), 'key': jax.random.normal(ks[1], (B, S, D_MODEL), jnp.float32), 'value': jax.random.normal(ks[2], (B, S, D_MODEL), jnp.float32), 'w_q': xavier(ks[3], (D_MODEL, D_MODEL)), 'b_q': jnp.zeros((D_MODEL,), jnp.float32), 'w_k': xavier(ks[4], (D_MODEL, D_MODEL)), 'b_k': jnp.zeros((D_MODEL,), jnp.float32), 'w_v': xavier(ks[5], (D_MODEL, D_MODEL)), 'b_v': jnp.zeros((D_MODEL,), jnp.float32), 'w_o': xavier(ks[6], (D_MODEL, D_MODEL)), 'b_o': jnp.zeros((D_MODEL,), jnp.float32)}
    _L0_xattn_all = _L0_xattn_setup()
    _L0_xattn_in = {k: v for k, v in _L0_xattn_all.items() if k in ('w_q', 'b_q', 'w_k', 'b_k', 'w_v', 'b_v', 'w_o', 'b_o')}
    del _L0_xattn_all

    def _L0_ffn_setup():
        import math
        import jax, jax.numpy as jnp
        import numpy as np
        NUM_EXPERTS = 16
        TOP_K = 2
        CAPACITY_FACTOR = 1.25
        key = jax.random.key(seed)
        k1, k2, k3, k4 = jax.random.split(key, 4)
        d, dff, E = (512, 2048, NUM_EXPERTS)
        x = jax.random.normal(k1, (4, 1024, d), dtype=jnp.float32)
        router_w = jax.random.normal(k2, (E, d), dtype=jnp.float32) * d ** (-0.5)
        router_b = jnp.zeros((E,), dtype=jnp.float32)
        w1 = jax.random.normal(k3, (E, d, dff), dtype=jnp.float32) * 0.02
        b1 = jnp.zeros((E, dff), dtype=jnp.float32)
        w2 = jax.random.normal(k4, (E, dff, d), dtype=jnp.float32) * 0.02
        b2 = jnp.zeros((E, d), dtype=jnp.float32)
        return {'x': x, 'router_w': router_w, 'router_b': router_b, 'w1': w1, 'b1': b1, 'w2': w2, 'b2': b2}
    _L0_ffn_all = _L0_ffn_setup()
    _L0_ffn_in = {k: v for k, v in _L0_ffn_all.items() if k in ('router_w', 'router_b', 'w1', 'b1', 'w2', 'b2')}
    del _L0_ffn_all
    return {'x': x, 'ctx_1024': ctx_1024, 'g_xattn': g_xattn, 'g_ffn': g_ffn, 'L0_xattn_w_q': _L0_xattn_in['w_q'], 'L0_xattn_b_q': _L0_xattn_in['b_q'], 'L0_xattn_w_k': _L0_xattn_in['w_k'], 'L0_xattn_b_k': _L0_xattn_in['b_k'], 'L0_xattn_w_v': _L0_xattn_in['w_v'], 'L0_xattn_b_v': _L0_xattn_in['b_v'], 'L0_xattn_w_o': _L0_xattn_in['w_o'], 'L0_xattn_b_o': _L0_xattn_in['b_o'], 'L0_ffn_router_w': _L0_ffn_in['router_w'], 'L0_ffn_router_b': _L0_ffn_in['router_b'], 'L0_ffn_w1': _L0_ffn_in['w1'], 'L0_ffn_b1': _L0_ffn_in['b1'], 'L0_ffn_w2': _L0_ffn_in['w2'], 'L0_ffn_b2': _L0_ffn_in['b2']}

def reference(x, ctx_1024, g_xattn, g_ffn, L0_xattn_w_q, L0_xattn_b_q, L0_xattn_w_k, L0_xattn_b_k, L0_xattn_w_v, L0_xattn_b_v, L0_xattn_w_o, L0_xattn_b_o, L0_ffn_router_w, L0_ffn_router_b, L0_ffn_w1, L0_ffn_b1, L0_ffn_w2, L0_ffn_b2):
    import jax
    import jax.numpy as jnp

    def _L0_xattn_ref(query, key, value, w_q, b_q, w_k, b_k, w_v, b_v, w_o, b_o):
        import jax, jax.numpy as jnp
        import numpy as np
        HEAD_NUM = 16
        D_MODEL = 512
        D_K = D_MODEL // HEAD_NUM
        B = query.shape[0]

        def proj(x, w, b):
            y = x @ w.T + b
            return y.reshape(B, -1, HEAD_NUM, D_K).transpose(0, 2, 1, 3)
        q = proj(query, w_q, b_q)
        k = proj(key, w_k, b_k)
        v = proj(value, w_v, b_v)
        scores = jnp.einsum('bhqd,bhkd->bhqk', q, k) / jnp.sqrt(jnp.float32(D_K))
        attn = jax.nn.softmax(scores, axis=-1)
        out = jnp.einsum('bhqk,bhkd->bhqd', attn, v)
        out = out.transpose(0, 2, 1, 3).reshape(B, -1, HEAD_NUM * D_K)
        return out @ w_o.T + b_o

    def _L0_ffn_ref(x, router_w, router_b, w1, b1, w2, b2):
        import math
        import jax, jax.numpy as jnp
        import numpy as np
        NUM_EXPERTS = 16
        TOP_K = 2
        CAPACITY_FACTOR = 1.25
        E, k = (NUM_EXPERTS, TOP_K)
        B, S, d = x.shape
        tokens = B * S
        capacity = max(1, int(math.ceil(CAPACITY_FACTOR * tokens * k / E)))
        x2d = x.reshape(tokens, d)
        logits = x2d @ router_w.T + router_b
        vals, idx = jax.lax.top_k(logits, k)
        gates = jax.nn.softmax(vals, axis=-1)
        flat_e = idx.reshape(-1)
        oh = (flat_e[:, None] == jnp.arange(E)[None, :]).astype(jnp.int32)
        pos = jnp.take_along_axis(jnp.cumsum(oh, axis=0) - 1, flat_e[:, None], axis=1)[:, 0]
        kept = pos < capacity
        kept2 = kept.reshape(tokens, k)
        denom = jnp.sum(gates * kept2, axis=-1, keepdims=True)
        gates = jnp.where(kept2, gates / (denom + 1e-09), 0.0)
        slot = flat_e * capacity + pos
        slot_safe = jnp.where(kept, slot, E * capacity)
        x_rep = jnp.repeat(x2d, k, axis=0)
        buf = jnp.zeros((E * capacity + 1, d), x.dtype).at[slot_safe].set(x_rep)
        packed = buf[:E * capacity].reshape(E, capacity, d)
        h = jax.nn.gelu(jnp.einsum('ecd,edf->ecf', packed, w1) + b1[:, None, :], approximate=False)
        expert_out = jnp.einsum('ecf,efd->ecd', h, w2) + b2[:, None, :]
        eflat = expert_out.reshape(E * capacity, d)
        gathered = eflat[jnp.clip(slot, 0, E * capacity - 1)]
        w = (gates.reshape(-1) * kept.astype(x.dtype))[:, None]
        out = (gathered * w).reshape(tokens, k, d).sum(axis=1)
        return out.reshape(B, S, d)
    x = x + jnp.tanh(g_xattn[0]) * _L0_xattn_ref(_layernorm(x, axis=-1), ctx_1024, ctx_1024, L0_xattn_w_q, L0_xattn_b_q, L0_xattn_w_k, L0_xattn_b_k, L0_xattn_w_v, L0_xattn_b_v, L0_xattn_w_o, L0_xattn_b_o)
    x = x + jnp.tanh(g_ffn[0]) * _L0_ffn_ref(_layernorm(x, axis=-1), L0_ffn_router_w, L0_ffn_router_b, L0_ffn_w1, L0_ffn_b1, L0_ffn_w2, L0_ffn_b2)
    return x

_drawn_inputs = setup_inputs


def setup_inputs(seed=0):
    import zlib

    import numpy as np

    out = dict(_drawn_inputs(seed))
    spreads = {'L0_xattn_b_q': (0.0, 0.1),
     'L0_xattn_b_k': (0.0, 0.1),
     'L0_xattn_b_v': (0.0, 0.1),
     'L0_xattn_b_o': (0.0, 0.1),
     'L0_ffn_router_b': (0.0, 0.1),
     'L0_ffn_b1': (0.0, 0.1),
     'L0_ffn_b2': (0.0, 0.1)}
    factors = {}
    for name, (base, spread) in spreads.items():
        noise = np.random.default_rng([zlib.crc32(name.encode()), seed]).standard_normal(out[name].shape)
        drawn = base * np.exp(spread * noise) if base else spread * noise
        out[name] = jnp.asarray(drawn.astype(out[name].dtype))
    for name, factor in factors.items():
        out[name] = (out[name] * factor).astype(out[name].dtype)
    return out
```

```python
import concourse.bass as bass
from concourse import mybir
from contextlib import ExitStack

F32 = mybir.dt.float32
F32R = mybir.dt.float32r
I32 = mybir.dt.int32
U32 = mybir.dt.uint32
ALU = mybir.AluOpType
ACT = mybir.ActivationFunctionType
AX = mybir.AxisListType

P = 128
D = 512
DC = D // P
H = 16
DH = D // H
HQ = P // DH
KEYS = 128
BATCH = 2
SEQ = 2048
TOK = BATCH * SEQ
GT = 512
TPG = GT // P
G = TOK // GT
GPB = SEQ // GT
NHALF = 2 * TPG
HH = H // 2
SCALE = DH ** -0.5
EPS = 1e-5

E = 16
F = 2048
FU = F // P
CAP = -(-5 * TOK * 2 // (4 * E))
ST = CAP // P
UPL = 2
PAIRS = FU // UPL
NRAW = 4
TABLE = (E + 1) * CAP
assert CAP % P == 0

SLOT_WORK = [[("O", 0)], [("O", 1)], [("x2T", 0), ("O", 2)], [("x2T", 1), ("O", 3)],
             [("x2T", 2), ("xT", 0)], [("x2T", 3), ("xT", 1)], [("xT", 2), ("lg", 0)], [("xT", 3)]]
END_WORK = [("q", c) for c in range(DC)] + [("rt", 0)] + [("pv", c) for c in range(DC)]
NEXT_GROUP = ("xT", "q")
LAST_GROUP = ("O", "x2T", "lg", "rt")
PREP_USES = 6
PROLOGUE_USES = TPG + DC
ALL_USES = sum(len(s) for s in SLOT_WORK) + len(END_WORK)


def uses_of(kinds_left_out):
    flat = [u for s in SLOT_WORK for u in s] + END_WORK
    return [u for u in flat if u[0] not in kinds_left_out]


class Work:

    def __init__(self, base, left_out=()):
        self.base, self.order = base, uses_of(left_out)

    def bank(self, use):
        return self.order.index(use) % 2

    def count(self, use):
        return self.base + self.order.index(use) + 1


def work_of(g):
    if isinstance(g, int) and g < 0:
        return Work(PREP_USES, ("O", "x2T", "lg", "rt", "pv"))
    if isinstance(g, int) and g == 0:
        return Work(PREP_USES + PROLOGUE_USES, LAST_GROUP)
    first = PREP_USES + PROLOGUE_USES + ALL_USES - 10
    left_out = ()
    if isinstance(g, int) and g == G - 1:
        left_out = NEXT_GROUP
    if isinstance(g, int) and g == G:
        return Work(first + (G - 1) * ALL_USES - PROLOGUE_USES, NEXT_GROUP + ("pv",))
    return Work((g - 1) * ALL_USES + first, left_out)


class Steps:

    def __init__(self, eng, sem):
        self.eng, self.sem, self.base, self.n = eng, sem, 0, 0

    def link(self, ins):
        self.n += 1
        ins.then_inc(self.sem, 1)
        self.eng.wait_ge(self.sem, self.base + self.n)

    def enter(self, base):
        self.base, self.n = base, 0


LINKS_LN = 14
LINKS_PROLOGUE = LINKS_LN
LINKS_FIRST = LINKS_LN + NHALF * 2
LINKS_ROUTE = 29
LINKS_MID = LINKS_FIRST + 2 * LINKS_LN + LINKS_ROUTE
LINKS_LAST = LINKS_MID - LINKS_LN


def build(nc, x, ctxT, gx, gf, wqT, bq, wkT, bk, wvT, bv, woT, bo, rwT, rb, w1, b1, w2, b2, out):
    xn_dram = nc.dram_tensor("xn_rows", [TOK + CAP, D], F32, kind="Internal").ap()
    table = nc.dram_tensor("slot_table", [TABLE + 2 * TOK, 2], I32, kind="Internal").ap()

    ctx = ExitStack()
    with ctx:
        def sem(name):
            return ctx.enter_context(nc.semaphore(name))

        psum = ctx.enter_context(nc.psum_tensor("banks", [P, 8, 512], F32))

        def wbank(b):
            return psum[:, 4 + b, :]

        ident = ctx.enter_context(nc.sbuf_tensor("ident", [P, P], F32))
        tgx = ctx.enter_context(nc.sbuf_tensor("tanh_gx", [P, 1], F32))
        tgf = ctx.enter_context(nc.sbuf_tensor("tanh_gf", [P, 1], F32))
        b1_sb = ctx.enter_context(nc.sbuf_tensor("b1_cols", [P, E * FU], F32))

        with ExitStack() as one:
            def sb(name, shape, dt=F32):
                return one.enter_context(nc.sbuf_tensor(name, shape, dt))

            before = sb("strict_upper", [P, P])
            ones = sb("ones", [P, P])
            iota_e = sb("iota_e", [P, E])
            iota_i = sb("iota_i", [P, E], I32)
            tok_i = sb("tok_i", [P, TPG], I32)
            trash_i = sb("trash_i", [P, 2, TPG], I32)
            tok_f = sb("tok_f", [P, TPG])
            trash_f = sb("trash_f", [P, 2, TPG])
            gates_in = sb("gates_in", [P, 2])
            bq_sb = sb("bq_sb", [P, DC])
            bk_sb = sb("bk_sb", [P, DC])
            bv_sb = sb("bv_sb", [P, D])
            bo_sb = sb("bo_sb", [P, D])
            rb_sb = sb("rb_sb", [P, E])
            rw_sb = sb("rw_sb", [P, DC, E])
            wq_h = sb("wq_h", [P, DC, D], F32R)
            wq_l = sb("wq_l", [P, DC, D], F32R)
            wo_h = sb("wo_h", [P, DC, D], F32R)
            wo_l = sb("wo_l", [P, DC, D], F32R)
            kbd_h = sb("kbd_h", [P, BATCH * DC * HQ * KEYS], F32R)
            kbd_l = sb("kbd_l", [P, BATCH * DC * HQ * KEYS], F32R)
            v_all = sb("v_all", [P, BATCH * D])
            v_cur = sb("v_cur", [P, D])
            x_sb = sb("x_sb", [P, TPG, D])
            xr = sb("xr", [P, TPG, D])
            xn = sb("xn", [P, 2, D])
            xnT_h = sb("xnT_h", [P, DC, GT], F32R)
            xnT_l = sb("xnT_l", [P, DC, GT], F32R)
            qT_h = sb("qT_h", [P, DC, GT], F32R)
            qT_l = sb("qT_l", [P, DC, GT], F32R)
            prob = sb("prob", [P, 2, HH, KEYS])
            probT = sb("probT", [P, H, GT])
            oT_h = sb("oT_h", [P, DC, GT], F32R)
            oT_l = sb("oT_l", [P, DC, GT], F32R)
            x2 = sb("x2", [P, 2, D])
            xn2 = sb("xn2", [P, 2, D])
            x2T = sb("x2T", [P, DC, GT])
            stats = sb("stats", [P, TPG, 6])
            mv = sb("mean_var", [P, TPG, 2])
            ve = sb("ve", [P, TPG])
            nhv = sb("neg_half_var", [P, TPG])
            rs = sb("rstd", [P, TPG])
            nt = sb("newton", [P, TPG])
            nmax = sb("nmax", [P, 2, HH])
            nbias = sb("nbias", [P, 2, HH])
            psums = sb("prob_sums", [P, 2, HH])
            rinv = sb("rinv", [P, 2, HH])
            logits = sb("logits", [P, TPG, E])
            top = sb("top", [P, TPG, 8])
            topi = sb("topi", [P, TPG, 8], U32)
            topf = sb("topf", [P, 2, TPG])
            onehot = sb("onehot", [P, 2, TPG, E])
            chosen = sb("chosen", [P, TPG, E])
            run = sb("running_base", [P, TPG + 1, E])
            pos = sb("pos", [P, TPG, E])
            prod = sb("prod", [P, 2, TPG, E])
            pk = sb("pk", [P, 2, TPG])
            kept = sb("kept", [P, 2, TPG])
            part = sb("part", [P, 2, TPG])
            dest_f = sb("dest_f", [P, 2, TPG])
            dest = sb("dest", [P, 2, TPG], I32)
            entry = sb("entry", [P, 2, TPG, 2], I32)
            vdiff = sb("vdiff", [P, TPG])
            gexp = sb("gexp", [P, TPG])
            gk = sb("gk", [P, 2, TPG])
            den = sb("den", [P, TPG])

        raw_w = [probT[:, 4 * i:4 * i + 4, :] for i in range(4)]
        ctx_sb = x2T[:, :, 0:BATCH * KEYS]
        fill = prob[:, :, :, :].rearrange("p a h k -> p (a h k)").bitcast(I32)

        with ExitStack() as two:
            def sb(name, shape, dt=F32):
                return two.enter_context(nc.sbuf_tensor(name, shape, dt))

            raw1 = sb("raw_w1", [P, NRAW, UPL * D])
            raw2 = sb("raw_w2", [P, NRAW, UPL * D])
            w1_h = sb("w1_h", [P, 4, DC, P], F32R)
            w1_l = sb("w1_l", [P, 4, DC, P], F32R)
            w2_h = sb("w2_h", [P, 4, D], F32R)
            w2_l = sb("w2_l", [P, 4, D], F32R)
            xg = sb("xg", [P, ST, D])
            xT_h = sb("xT_h", [P, DC, CAP], F32R)
            xT_l = sb("xT_l", [P, DC, CAP], F32R)
            h_f = sb("h_f", [P, 3, CAP])
            h_h = sb("h_h", [P, 3, CAP], F32R)
            h_l = sb("h_l", [P, 3, CAP], F32R)
            y_sb = sb("y_sb", [P, ST, D])
            y_w = sb("y_w", [P, ST, D])
            b2_sb = sb("b2_sb", [P, D])
            b1_cur = sb("b1_cur", [P, FU])
            tab_next = sb("tab_next", [P, ST, 2], I32)
            tab_cur = sb("tab_cur", [P, ST, 2], I32)

        const_done = sem("const_done")
        w_loaded = sem("w_loaded")
        small_loaded = sem("small_loaded")
        w_hi = sem("w_hi")
        kbd_ready = sem("kbd_ready")
        bo_ready = sem("bo_ready")
        tanh_done = sem("tanh_done")
        fill_ready = sem("fill_ready")
        init_stored = sem("init_stored")
        x_loaded = sem("x_loaded")
        xr_loaded = sem("xr_loaded")
        xr_ready = sem("xr_ready")
        dve_step = sem("dve_step")
        xn_ready = sem("xn_ready")
        work_filled = sem("work_filled")
        work_drained = sem("work_drained")
        xT_hi = sem("xT_hi")
        q_hi = sem("q_hi")
        o_hi = sem("o_hi")
        s_filled = sem("s_filled")
        nbias_ready = sem("nbias_ready")
        exp_done = sem("exp_done")
        prob_ready = sem("prob_ready")
        pT_filled = sem("pT_filled")
        pT_act = sem("pT_act")
        pT_dve = sem("pT_dve")
        v_ready = sem("v_ready")
        xn2_ready = sem("xn2_ready")
        x2_stored = [sem(f"x2_stored{i}") for i in range(2)]
        xn2_stored = [sem(f"xn2_stored{i}") for i in range(2)]
        chosen_ready = sem("chosen_ready")
        vdiff_ready = sem("vdiff_ready")
        gexp_done = sem("gexp_done")
        entry_ready = sem("entry_ready")
        scattered = sem("scattered")
        entry_free = sem("entry_free")
        phase1_done = sem("phase1_done")

        raw_loaded = [sem(f"raw_loaded{i}") for i in range(NRAW)]
        w1_hi = sem("w1_hi")
        w1_split = sem("w1_split")
        w2_hi = sem("w2_hi")
        w2_split = sem("w2_split")
        tab_loaded = sem("tab_loaded")
        tab_taken = sem("tab_taken")
        gathered = [sem(f"gathered{i}") for i in range(ST)]
        xg_turned = sem("xg_turned")
        xg_hi = sem("xg_hi")
        xg_split = sem("xg_split")
        h_filled = sem("h_filled")
        h_gelu = sem("h_gelu")
        h_split = sem("h_split")
        down_done = sem("down_done")
        y_filled = sem("y_filled")
        y_biased = sem("y_biased")
        y_weighted = sem("y_weighted")
        b2_loaded = sem("b2_loaded")
        added = sem("added")
        passed = sem("passed")
        b1_taken = sem("b1_taken")

        def wait_apart(eng, s, value):
            eng.wait_ge(s, value)
            eng.sem_inc(passed, 1)

        def first_wait(eng, s, value):
            if not isinstance(value, int) or value > 0:
                eng.wait_ge(s, value)

        def rows_of(t, g):
            return t[bass.ds(g * GT, GT), :].rearrange("(t p) n -> p t n", p=P)

        block = ctx.enter_context(nc.Block())

        @block.sync
        def _(sp):
            sp.dma_start(ctx_sb, ctxT.rearrange("(c p) n -> p c n", p=P)).then_inc(w_loaded, 16)
            for i, w in enumerate((wqT, wkT, wvT, woT)):
                sp.dma_start(raw_w[i], w.rearrange("(c p) n -> p c n", p=P)).then_inc(w_loaded, 16)
            sp.dma_start(x_sb[:], rows_of(x, 0)).then_inc(x_loaded, 16)
            sp.dma_start(rw_sb[:], rwT.rearrange("(c p) n -> p c n", p=P)).then_inc(small_loaded, 16)
            sp.dma_start(bq_sb[:], bq).then_inc(small_loaded, 16)
            sp.dma_start(bk_sb[:], bk).then_inc(small_loaded, 16)
            for dst, src in ((bv_sb[:], bv), (bo_sb[:], bo), (rb_sb[:], rb),
                             (gates_in[:, 0:1], gx), (gates_in[:, 1:2], gf)):
                sp.dma_start(dst, src.broadcast_to(list(dst.shape))).then_inc(small_loaded, 16)
            sp.dma_start(b1_sb[:], b1).then_inc(small_loaded, 16)
            sp.dma_start(xr[:], rows_of(x, 0)).then_inc(xr_loaded, 16)
            sp.wait_ge(fill_ready, 2)
            sp.dma_start(table[0:TABLE, :].rearrange("(e s) w -> e (s w)", s=CAP),
                         fill[0:E + 1, 0:2 * CAP]).then_inc(init_stored, 16)
            for i in range(ST):
                rows = slice(TOK + i * P, TOK + (i + 1) * P)
                sp.dma_start(xn_dram[rows, :], x2[:, 0, :]).then_inc(init_stored, 16)
                sp.dma_start(out[rows, :], x2[:, 0, :]).then_inc(init_stored, 16)

            def loads_and_stores(g):
                w = work_of(g)
                first, last, past = (isinstance(g, int) and g == v for v in (0, G - 1, G))
                if not (last or past):
                    sp.wait_ge(xn_ready, TPG * g + TPG)
                    sp.dma_start(x_sb[:], rows_of(x, g + 1)).then_inc(x_loaded, 16)
                if not first:
                    for t in range(TPG):
                        rows = bass.ds((g - 1) * GT + t * P, P)
                        sp.wait_ge(work_drained, w.count(("O", t)))
                        sp.dma_start(out[rows, :], x2[:, t % 2, :]).then_inc(x2_stored[t % 2], 16)
                        if t % 2:
                            for u in (t - 1, t):
                                rows = bass.ds((g - 1) * GT + u * P, P)
                                sp.wait_ge(xn2_ready, (g - 1) * TPG + u + 1)
                                sp.dma_start(xn_dram[rows, :], xn2[:, u % 2, :])\
                                    .then_inc(xn2_stored[u % 2], 16)
                    for i in range(2):
                        sp.wait_ge(x2_stored[i], g * (16 * TPG // 2))
                        sp.wait_ge(xn2_stored[i], g * (16 * TPG // 2))
                    if not past:
                        sp.dma_start(xr[:], rows_of(x, g)).then_inc(xr_loaded, 16)

            loads_and_stores(0)
            with sp.Fori(1, G - 1) as g:
                loads_and_stores(g)
            loads_and_stores(G - 1)
            loads_and_stores(G)

            sp.wait_ge(phase1_done, 3)

            def load_weights(e, pair, turn):
                r = pair % NRAW
                if turn is not None:
                    sp.wait_ge(w1_split, turn)
                    sp.wait_ge(w2_split, turn)
                src = bass.ds(e * PAIRS + pair, 1)
                sp.dma_start(raw1[:, r, :], w1[src].rearrange("a p n -> p (a n)")).then_inc(raw_loaded[r], 16)
                sp.dma_start(raw2[:, r, :], w2[src].rearrange("a p n -> p (a n)")).then_inc(raw_loaded[r], 16)

            for pair in range(NRAW):
                load_weights(0, pair, None)
            with sp.Fori(0, E - 1) as e:
                for pair in range(PAIRS):
                    ahead = pair + NRAW
                    load_weights(e + ahead // PAIRS, ahead % PAIRS, e * FU + UPL * (pair + 1))
                    if pair == NRAW:
                        sp.dma_start(b2_sb[:], b2[bass.ds(e, 1), :].broadcast_to([P, D])).then_inc(b2_loaded, 16)
            for pair in range(PAIRS - NRAW):
                load_weights(E - 1, pair + NRAW, (E - 1) * FU + UPL * (pair + 1))
            load_weights(E - 1, 0, (E - 1) * FU + UPL * (PAIRS - NRAW + 1))
            sp.dma_start(b2_sb[:], b2[E - 1:E, :].broadcast_to([P, D])).then_inc(b2_loaded, 16)
            sp.wait_ge(added, 16 * E * ST)

        @block.gpsimd
        def _(pool):
            pool.memset(ident[:], 0.0).then_inc(const_done, 1)
            pool.memset(before[:], 0.0).then_inc(const_done, 1)
            pool.memset(ones[:], 1.0).then_inc(const_done, 1)
            pool.wait_ge(const_done, 3)
            pool.affine_select(out=ident[:], in_=ident[:], compare_op=ALU.not_equal, fill=1.0, base=0,
                               pattern=[[-1, P]], channel_multiplier=1).then_inc(const_done, 1)
            pool.affine_select(out=before[:], in_=before[:], compare_op=ALU.is_ge, fill=1.0, base=0,
                               pattern=[[-1, P]], channel_multiplier=1).then_inc(const_done, 1)
            pool.iota(iota_i[:], pattern=[[1, E]], base=0, channel_multiplier=0).then_inc(const_done, 1)
            pool.iota(tok_i[:], pattern=[[P, TPG]], base=0, channel_multiplier=1).then_inc(const_done, 1)
            pool.iota(trash_i[:], pattern=[[TOK, 2], [P, TPG]], base=TABLE, channel_multiplier=1)\
                .then_inc(const_done, 1)
            pool.memset(x2[:, 0, :], 0.0).then_inc(fill_ready, 1)
            pool.memset(fill[0:E + 1, 0:2 * CAP], 0).then_inc(const_done, 1)
            pool.wait_ge(const_done, 9)
            pool.iota(fill[0:E + 1, 0:2 * CAP:2], pattern=[[1, CAP]], base=TOK, channel_multiplier=0)\
                .then_inc(fill_ready, 1)

            def add_bo(g):
                pool.wait_ge(xr_loaded, 16 * g + 16)
                pool.tensor_tensor(xr[:], xr[:], bo_sb[:, None, :].broadcast_to([P, TPG, D]), ALU.add)\
                    .then_inc(xr_ready, 1)

            def scatter(g):
                wait_apart(pool, entry_ready, g + 1)
                for k in range(2):
                    for t in range(TPG):
                        pool.indirect_dma_start(
                            out=table[:, :], out_offset=bass.IndirectOffsetOnAxis(ap=dest[:, k, t:t + 1], axis=0),
                            in_=entry[:, k, t, :], in_offset=None).then_inc(scattered, 16)
                pool.wait_ge(scattered, (g + 1) * (16 * 2 * TPG))

            pool.wait_ge(bo_ready, 1)
            pool.wait_ge(init_stored, 16 * (1 + 2 * ST))
            add_bo(0)
            pool.sem_inc(entry_free, 1)
            add_bo(1)
            with pool.Fori(2, G) as g:
                scatter(g - 2)
                pool.sem_inc(entry_free, 1)
                add_bo(g)
            scatter(G - 2)
            pool.sem_inc(entry_free, 1)
            scatter(G - 1)
            pool.wait_ge(phase1_done, 3)
            for i in range(2):
                pool.wait_ge(x2_stored[i], 16 * TPG // 2 * G)
                pool.wait_ge(xn2_stored[i], 16 * TPG // 2 * G)

            def load_table(e):
                pool.dma_start(tab_next[:], table[bass.ds(e * CAP, CAP), :].rearrange("(p i) w -> p i w", i=ST))\
                    .then_inc(tab_loaded, 16)

            def gather(e):
                wait_apart(pool, tab_loaded, 16 * e + 16)
                for i in range(ST):
                    pool.indirect_dma_start(
                        out=xg[:, i, :], out_offset=None, in_=xn_dram[:, :],
                        in_offset=bass.IndirectOffsetOnAxis(ap=tab_next[:, i, 0:1], axis=0))\
                        .then_inc(gathered[i], 16)

            load_table(0)
            gather(0)
            with pool.Fori(0, E) as e:
                pool.tensor_copy(tab_cur[:], tab_next[:]).then_inc(tab_taken, 1)
                pool.wait_ge(tab_taken, e + 1)
                for i in range(ST):
                    pool.wait_ge(gathered[i], 16 * e + 16)
                load_table(e + 1)
                pool.wait_ge(xg_turned, ST * (e + 1))
                gather(e + 1)
                for i in range(ST):
                    wait_apart(pool, y_weighted, e * ST + i + 1)
                    pool.indirect_dma_start(
                        out=out[:, :], out_offset=bass.IndirectOffsetOnAxis(ap=tab_cur[:, i, 0:1], axis=0),
                        in_=y_w[:, i, :], in_offset=None, compute_op=ALU.add).then_inc(added, 16)
                    pool.wait_ge(added, 16 * (e * ST + i + 1))
            for i in range(ST):
                pool.wait_ge(gathered[i], 16 * (E + 1))

        @block.scalar
        def _(act):
            act.wait_ge(small_loaded, 16 * 9)
            act.activation(tgx[:], gates_in[:, 0:1], ACT.Tanh).then_inc(tanh_done, 1)
            act.activation(tgf[:], gates_in[:, 1:2], ACT.Tanh).then_inc(tanh_done, 1)
            act.wait_ge(w_loaded, 16 * 5)
            for c in range(DC):
                act.wait_ge(work_filled, c + 1)
                act.activation(xnT_h[:, c, 0:BATCH * KEYS], wbank(c % 2)[:, 0:BATCH * KEYS], ACT.Identity,
                               bias=bk_sb[:, c:c + 1]).then_inc(w_hi, 1)
            act.activation(wq_h[:], raw_w[0], ACT.Copy).then_inc(w_hi, 1)
            act.activation(wo_h[:], raw_w[3], ACT.Copy).then_inc(w_hi, 1)
            act.wait_ge(kbd_ready, 1)

            def x_hi(w, t):
                act.wait_ge(work_filled, w.count(("xT", t)))
                act.activation(xnT_h[:, :, t * P:(t + 1) * P],
                               wbank(w.bank(("xT", t))).rearrange("p (c n) -> p c n", c=DC), ACT.Copy)\
                    .then_inc(xT_hi, 1)

            def query_hi(w, c):
                act.wait_ge(work_filled, w.count(("q", c)))
                act.activation(qT_h[:, c, :], wbank(w.bank(("q", c))), ACT.Identity,
                               bias=bq_sb[:, c:c + 1]).then_inc(q_hi, 1)

            def exps(g, j):
                act.wait_ge(nbias_ready, NHALF * g + j + 1)
                first_wait(act, pT_filled, NHALF * g + j - 1)
                for h in range(HH):
                    ins = act.activation(prob[:, j % 2, h, :],
                                         psum[:, 2 * (j % 2) + h // HQ, (h % HQ) * KEYS:(h % HQ + 1) * KEYS],
                                         ACT.Exp, bias=nbias[:, j % 2, h:h + 1], scale=SCALE,
                                         accum_out=psums[:, j % 2, h:h + 1])
                ins.then_inc(exp_done, 1)

            def take_pT(g, j):
                act.wait_ge(pT_filled, NHALF * g + j + 1)
                h0, t = (j % 2) * HH, j // 2
                act.activation(probT[:, h0:h0 + HQ, t * P:(t + 1) * P],
                               psum[:, 6, :].rearrange("p (h n) -> p h n", h=HQ), ACT.Copy).then_inc(pT_act, 1)

            def step(g):
                w = work_of(g)
                first, last, past = (isinstance(g, int) and g == v for v in (0, G - 1, G))
                if not past:
                    for j in range(NHALF):
                        exps(g, j)
                        if j >= 2:
                            take_pT(g, j - 2)
                        for kind, t in SLOT_WORK[j]:
                            if kind == "xT" and not last:
                                x_hi(w, t)
                if not (last or past):
                    query_hi(w, 0)
                    query_hi(w, 1)
                if not past:
                    take_pT(g, NHALF - 2)
                if not (last or past):
                    query_hi(w, 2)
                    query_hi(w, 3)
                if not past:
                    take_pT(g, NHALF - 1)
                if not first:
                    act.wait_ge(vdiff_ready, g)
                    act.activation(gexp[:], vdiff[:], ACT.Exp).then_inc(gexp_done, 1)
                if not past:
                    for c in range(DC):
                        act.wait_ge(work_filled, w.count(("pv", c)))
                        act.activation(oT_h[:, c, :], wbank(w.bank(("pv", c))), ACT.Copy).then_inc(o_hi, 1)

            w = work_of(-1)
            for t in range(TPG):
                x_hi(w, t)
            for c in range(DC):
                query_hi(w, c)
            act.wait_ge(init_stored, 16 * (1 + 2 * ST))
            step(0)
            with act.Fori(1, G - 1) as g:
                step(g)
            step(G - 1)
            step(G)
            act.drain().then_inc(phase1_done, 1)
            act.wait_ge(phase1_done, 3)

            def weights_hi(u, e):
                pair, r = (u // UPL) % PAIRS, (u // UPL) % NRAW
                n = u % UPL
                act.wait_ge(raw_loaded[r], e * (32 * PAIRS // NRAW) + 32 * ((u // UPL) // NRAW + 1))
                act.activation(w1_h[:, u % 4], raw1[:, r, n * D:(n + 1) * D].rearrange("p (c n) -> p c n", c=DC),
                               ACT.Copy).then_inc(w1_hi, 1)
                if u >= 4:
                    act.wait_ge(down_done, e * (FU - 1) + u - 3)
                act.activation(w2_h[:, u % 4], raw2[:, r, n * D:(n + 1) * D], ACT.Copy).then_inc(w2_hi, 1)

            def rows_hi(e, i):
                act.wait_ge(xg_turned, e * ST + i + 1)
                act.activation(xT_h[:, :, i * P:(i + 1) * P],
                               psum[:, 5 + i % 3, :].rearrange("p (c n) -> p c n", c=DC), ACT.Copy)\
                    .then_inc(xg_hi, 1)

            weights_hi(0, 0)
            weights_hi(1, 0)
            for i in range(ST):
                rows_hi(0, i)
            with act.Fori(0, E) as e:
                act.wait_ge(b1_taken, e + 1)
                for u in range(FU):
                    weights_hi(u + 2, e)
                    for half in range(2):
                        n = 2 * u + half
                        cols = slice(half * CAP // 2, (half + 1) * CAP // 2)
                        act.wait_ge(h_filled, e * (2 * FU) + n + 1)
                        hp = psum[:, 5 + n % 3, 0:CAP // 2]
                        bias = b1_cur[:, u:u + 1]
                        act.activation(h_f[:, u % 3, cols], hp, ACT.Gelu, bias=bias)
                        act.activation(h_h[:, u % 3, cols], hp, ACT.Gelu, bias=bias).then_inc(h_gelu, 1)
                    if u == FU - 1:
                        for i in range(ST):
                            rows_hi(e + 1, i)
                act.wait_ge(tab_taken, e + 1)
                for i in range(ST):
                    act.wait_ge(y_biased, e * ST + i + 1)
                    act.activation(y_w[:, i, :], y_sb[:, i, :], ACT.Copy,
                                   scale=tab_cur[:, i, 1:2].bitcast(F32)).then_inc(y_weighted, 1)

        @block.tensor
        def _(pe):
            def product(dst, pairs, cols=None):
                n = len(pairs)
                for i, (ah, al, bh, bl) in enumerate(pairs):
                    pe.matmul(dst, ah, bh, start=(i == 0), stop=False)
                    pe.matmul(dst, ah, bl, start=False, stop=False)
                    ins = pe.matmul(dst, al, bh, start=False, stop=(i == n - 1))
                return ins

            def take(w, use):
                pe.wait_ge(work_drained, w.count(use) - 2)
                return wbank(w.bank(use))

            pe.wait_ge(w_loaded, 16 * 5)
            for c in range(DC):
                if c >= 2:
                    pe.wait_ge(work_drained, c - 1)
                for i in range(DC):
                    ins = pe.matmul(wbank(c % 2)[:, 0:BATCH * KEYS], raw_w[1][:, i, c * P:(c + 1) * P],
                                    ctx_sb[:, i, :], start=(i == 0), stop=(i == DC - 1))
                ins.then_inc(work_filled, 1)
            for b in range(BATCH):
                pe.wait_ge(work_drained, DC + b - 1)
                for i in range(DC):
                    ins = pe.matmul(wbank(b), ctx_sb[:, i, b * KEYS:(b + 1) * KEYS], raw_w[2][:, i, :],
                                    start=(i == 0), stop=(i == DC - 1))
                ins.then_inc(work_filled, 1)
            pe.wait_ge(const_done, 9)

            def turn_x(w, g, t):
                pe.wait_ge(xn_ready, TPG * g + t + 1)
                dst = take(w, ("xT", t))
                for c in range(DC):
                    ins = pe.transpose(dst[:, c * P:(c + 1) * P], xn[:, t % 2, c * P:(c + 1) * P], ident[:])
                ins.then_inc(work_filled, 1)

            def query(w, c):
                if c == 0:
                    pe.wait_ge(work_drained, w.count(("xT", TPG - 1)))
                dst = take(w, ("q", c))
                cs = slice(c * P, (c + 1) * P)
                product(dst, [(wq_h[:, i, cs], wq_l[:, i, cs], xnT_h[:, i, :], xnT_l[:, i, :])
                              for i in range(DC)]).then_inc(work_filled, 1)

            def scores(g, j):
                first_wait(pe, exp_done, NHALF * g + j - 1)
                t = j // 2
                ts = slice(t * P, (t + 1) * P)
                for n in range(2):
                    c = 2 * (j % 2) + n
                    off = (g // GPB) * (DC * HQ * KEYS) + c * HQ * KEYS
                    kh, kl = (k[:, bass.ds(off, HQ * KEYS)] for k in (kbd_h, kbd_l))
                    ins = product(psum[:, 2 * (j % 2) + n, :], [(qT_h[:, c, ts], qT_l[:, c, ts], kh, kl)])
                ins.then_inc(s_filled, 1)

            def turn_probs(g, j):
                pe.wait_ge(prob_ready, NHALF * g + j + 1)
                first_wait(pe, pT_act, NHALF * g + j)
                first_wait(pe, pT_dve, NHALF * g + j)
                for h in range(HH):
                    ins = pe.transpose(psum[:, 6 + h // HQ, (h % HQ) * P:(h % HQ + 1) * P],
                                       prob[:, j % 2, h, :], ident[:])
                ins.then_inc(pT_filled, 1)

            def context(w, g, c):
                if c == 0:
                    pe.wait_ge(pT_act, NHALF * (g + 1))
                    pe.wait_ge(pT_dve, NHALF * (g + 1))
                    pe.wait_ge(v_ready, g + 1)
                dst = take(w, ("pv", c))
                for n in range(HQ):
                    h = HQ * c + n
                    ins = pe.matmul(dst[n * DH:(n + 1) * DH, :], v_cur[:, h * DH:(h + 1) * DH], probT[:, h, :],
                                    start=True, stop=True)
                ins.then_inc(work_filled, 1)

            def project(w, before_w, t):
                if t == 0:
                    pe.wait_ge(work_drained, before_w.count(("pv", DC - 1)))
                dst = take(w, ("O", t))
                ts = slice(t * P, (t + 1) * P)
                product(dst, [(oT_h[:, c, ts], oT_l[:, c, ts], wo_h[:, c, :], wo_l[:, c, :])
                              for c in range(DC)]).then_inc(work_filled, 1)

            def turn_x2(w, g, t):
                pe.wait_ge(xn2_ready, TPG * (g - 1) + t + 1)
                dst = take(w, ("x2T", t))
                for c in range(DC):
                    ins = pe.transpose(dst[:, c * P:(c + 1) * P], xn2[:, t % 2, c * P:(c + 1) * P], ident[:])
                ins.then_inc(work_filled, 1)

            def route_logits(w):
                pe.wait_ge(work_drained, w.count(("x2T", TPG - 1)))
                dst = take(w, ("lg", 0))
                for t in range(TPG):
                    for c in range(DC):
                        ins = pe.matmul(dst[:, t * E:(t + 1) * E], x2T[:, c, t * P:(t + 1) * P], rw_sb[:, c, :],
                                        start=(c == 0), stop=(c == DC - 1))
                ins.then_inc(work_filled, 1)

            def count_chosen(w, g):
                pe.wait_ge(chosen_ready, g)
                dst = take(w, ("rt", 0))
                m = chosen[:].rearrange("p t e -> p (t e)")
                pe.matmul(dst[:, 0:TPG * E], before[:], m, start=True, stop=True)
                pe.matmul(dst[:, TPG * E:2 * TPG * E], ones[:], m, start=True, stop=True).then_inc(work_filled, 1)

            def step(g):
                w = work_of(g)
                before_w = work_of(g - 1) if not isinstance(g, int) or g > 0 else None
                if not isinstance(g, int):
                    before_w = Work(w.base - ALL_USES)
                first, last, past = (isinstance(g, int) and g == v for v in (0, G - 1, G))
                for j in range(NHALF):
                    if not past:
                        if j == 0:
                            qw = work_of(-1) if first else before_w
                            pe.wait_ge(work_drained, qw.count(("q", DC - 1)))
                        scores(g, j)
                        if j >= 2:
                            turn_probs(g, j - 2)
                    for kind, t in SLOT_WORK[j]:
                        if kind == "O" and not first:
                            project(w, before_w, t)
                        if kind == "x2T" and not first:
                            turn_x2(w, g, t)
                        if kind == "lg" and not first:
                            route_logits(w)
                        if kind == "xT" and not (last or past):
                            turn_x(w, g + 1, t)
                more = not (last or past)
                if more:
                    query(w, 0)
                    query(w, 1)
                if not past:
                    turn_probs(g, NHALF - 2)
                if more:
                    query(w, 2)
                    query(w, 3)
                if not past:
                    turn_probs(g, NHALF - 1)
                if not first:
                    count_chosen(w, g)
                if not past:
                    for c in range(DC):
                        context(w, g, c)

            w = work_of(-1)
            for t in range(TPG):
                turn_x(w, 0, t)
            pe.wait_ge(w_hi, DC + 2)
            pe.wait_ge(kbd_ready, 3)
            for c in range(DC):
                query(w, c)
            step(0)
            with pe.Fori(1, G - 1) as g:
                step(g)
            step(G - 1)
            step(G)
            pe.drain().then_inc(phase1_done, 1)
            pe.wait_ge(phase1_done, 3)

            def turn_rows(e):
                for i in range(ST):
                    pe.wait_ge(gathered[i], 16 * e + 16)
                    if i < 3:
                        first_wait(pe, h_split, e * (2 * FU))
                    else:
                        pe.wait_ge(xg_split, e * ST + i - 2)
                    for c in range(DC):
                        ins = pe.transpose(psum[:, 5 + i % 3, c * P:(c + 1) * P], xg[:, i, c * P:(c + 1) * P],
                                           ident[:])
                    ins.then_inc(xg_turned, 1)

            def up(e, u):
                pe.wait_ge(w1_split, e * FU + u + 1)
                for half in range(2):
                    n = 2 * u + half
                    cols = slice(half * CAP // 2, (half + 1) * CAP // 2)
                    if n < 3:
                        pe.wait_ge(xg_split, (e + 1) * ST)
                    else:
                        pe.wait_ge(h_split, e * (2 * FU) + n - 2)
                    ins = product(psum[:, 5 + n % 3, 0:CAP // 2],
                                  [(w1_h[:, u % 4, c, :], w1_l[:, u % 4, c, :], xT_h[:, c, cols], xT_l[:, c, cols])
                                   for c in range(DC)])
                    ins.then_inc(h_filled, 1)

            def down(e, u):
                pe.wait_ge(w2_split, e * FU + u + 1)
                pe.wait_ge(h_split, e * (2 * FU) + 2 * u + 2)
                wh, wl = w2_h[:, u % 4, :], w2_l[:, u % 4, :]
                for i in range(ST):
                    rows = slice(i * P, (i + 1) * P)
                    hh, hl = h_h[:, u % 3, rows], h_l[:, u % 3, rows]
                    y = psum[:, i, :]
                    pe.matmul(y, hh, wh, start=(u == 0), stop=False)
                    pe.matmul(y, hh, wl, start=False, stop=False)
                    ins = pe.matmul(y, hl, wh, start=False, stop=(u == FU - 1))
                    if u == FU - 1:
                        ins.then_inc(y_filled, 1)
                if u < FU - 1:
                    ins.then_inc(down_done, 1)

            turn_rows(0)
            with pe.Fori(0, E) as e:
                up(e, 0)
                up(e, 1)
                for u in range(FU):
                    if u == FU - 1:
                        turn_rows(e + 1)
                    down(e, u)
                    if u + 2 < FU:
                        up(e, u + 2)

        @block.vector
        def _(dve):
            steps = Steps(dve, dve_step)
            link = steps.link

            def f32(ap):
                return ap.bitcast(F32)

            dve.memset(f32(kbd_h[:]), 0.0)
            link(dve.memset(f32(kbd_l[:]), 0.0))
            dve.memset(run[:, 0, :], 0.0)
            dve.wait_ge(const_done, 9)
            dve.tensor_copy(iota_e[:], iota_i[:])
            dve.tensor_copy(tok_f[:], tok_i[:])
            link(dve.tensor_copy(trash_f[:], trash_i[:]))
            for c in range(DC):
                dve.wait_ge(w_hi, c + 1)
                dve.scalar_tensor_tensor(out=xnT_l[:, c, 0:BATCH * KEYS], in0=wbank(c % 2)[:, 0:BATCH * KEYS],
                                         scalar=bk_sb[:, c:c + 1], in1=f32(xnT_h[:, c, 0:BATCH * KEYS]),
                                         op0=ALU.add, op1=ALU.subtract).then_inc(work_drained, 1)
            for b in range(BATCH):
                dve.wait_ge(work_filled, DC + b + 1)
                dve.tensor_tensor(v_all[:, b * D:(b + 1) * D], wbank(b), bv_sb[:], ALU.add)\
                    .then_inc(work_drained, 1)
            dve.wait_ge(work_drained, PREP_USES)
            for n in range(HQ):
                rows = slice(n * DH, (n + 1) * DH)
                for src, dst in ((xnT_h, kbd_h), (xnT_l, kbd_l)):
                    ins = dve.tensor_copy(
                        dst[rows, :].rearrange("p (b c h k) -> p b c h k", b=BATCH, c=DC, h=HQ)[:, :, :, n, :],
                        f32(src[rows, :, 0:BATCH * KEYS]).rearrange("p c (b k) -> p b c k", b=BATCH))
            ins.then_inc(kbd_ready, 1)
            dve.wait_ge(w_hi, DC + 2)
            dve.tensor_tensor(wq_l[:], raw_w[0], f32(wq_h[:]), ALU.subtract).then_inc(kbd_ready, 1)
            dve.tensor_tensor(wo_l[:], raw_w[3], f32(wo_h[:]), ALU.subtract).then_inc(kbd_ready, 1)
            dve.wait_ge(tanh_done, 2)
            dve.tensor_scalar(bo_sb[:], bo_sb[:], tgx[:, 0:1], None, ALU.mult).then_inc(bo_ready, 1)
            assert steps.n == 2, steps.n
            steps.enter(2)

            def norm_stats(src, t0, n):
                a, b = t0, t0 + n
                for t in range(a, b):
                    ins = dve.bn_stats(stats[:, t, :], src(t))
                link(ins)
                dve.sem_inc(passed, 1)
                for t in range(a, b):
                    ins = dve.bn_aggr(mv[:, t, :], stats[:, t, :])
                link(ins)
                link(dve.tensor_scalar(ve[:, a:b], mv[:, a:b, 1], EPS, None, ALU.add))
                dve.tensor_scalar(nhv[:, a:b], ve[:, a:b], -0.5, None, ALU.mult)
                link(dve.tensor_scalar(nt[:, a:b].bitcast(I32), ve[:, a:b].bitcast(I32), 1, None,
                                       ALU.logical_shift_right))
                link(dve.tensor_scalar(rs[:, a:b].bitcast(I32), nt[:, a:b].bitcast(I32), -1.0, 1597463007.0,
                                       ALU.mult, ALU.add))
                for r in range(3):
                    link(dve.tensor_tensor(nt[:, a:b], rs[:, a:b], rs[:, a:b], ALU.mult))
                    link(dve.tensor_tensor(nt[:, a:b], nt[:, a:b], nhv[:, a:b], ALU.mult))
                    ins = dve.scalar_tensor_tensor(out=rs[:, a:b], in0=nt[:, a:b], scalar=1.5, in1=rs[:, a:b],
                                                   op0=ALU.add, op1=ALU.mult)
                    if r < 2:
                        link(ins)
                link(ins)

            def normalise(dst, src, t):
                return dve.tensor_scalar(dst, src, mv[:, t, 0:1], rs[:, t:t + 1], ALU.subtract, ALU.mult)

            def x_stats(g):
                dve.wait_ge(x_loaded, 16 * g + 16)
                norm_stats(lambda t: x_sb[:, t, :], 0, TPG)

            def x_norm(t):
                normalise(xn[:, t % 2, :], x_sb[:, t, :], t).then_inc(xn_ready, 1)

            def x_lo(w, g, t):
                dve.wait_ge(xT_hi, TPG * g + t + 1)
                ts = slice(t * P, (t + 1) * P)
                dve.tensor_tensor(xnT_l[:, :, ts], wbank(w.bank(("xT", t))).rearrange("p (c n) -> p c n", c=DC),
                                  f32(xnT_h[:, :, ts]), ALU.subtract).then_inc(work_drained, 1)

            def query_lo(w, g, c):
                dve.wait_ge(q_hi, DC * g + c + 1)
                dve.scalar_tensor_tensor(out=qT_l[:, c, :], in0=wbank(w.bank(("q", c))),
                                         scalar=bq_sb[:, c:c + 1], in1=f32(qT_h[:, c, :]),
                                         op0=ALU.add, op1=ALU.subtract).then_inc(work_drained, 1)

            def row_max(g, j):
                b = j % 2
                dve.wait_ge(s_filled, NHALF * g + j + 1)
                link(dve.tensor_reduce(nmax[:, b, :].rearrange("p (a h) -> p a h", a=2),
                                       psum[:, 2 * b:2 * b + 2, :].rearrange("p a (h k) -> p a h k", h=HQ),
                                       AX.X, ALU.max, negate=True))
                dve.tensor_scalar(nbias[:, b, :], nmax[:, b, :], SCALE, None, ALU.mult).then_inc(nbias_ready, 1)

            def softmax_norm(g, j):
                b = j % 2
                dve.wait_ge(exp_done, NHALF * g + j + 1)
                link(dve.reciprocal(rinv[:, b, :], psums[:, b, :]))
                dve.tensor_tensor(prob[:, b], prob[:, b], rinv[:, b, :, None].broadcast_to([P, HH, KEYS]),
                                  ALU.mult).then_inc(prob_ready, 1)

            def take_pT(g, j):
                dve.wait_ge(pT_filled, NHALF * g + j + 1)
                h0, t = (j % 2) * HH + HQ, j // 2
                dve.tensor_copy(probT[:, h0:h0 + HQ, t * P:(t + 1) * P],
                                psum[:, 7, :].rearrange("p (h n) -> p h n", h=HQ)).then_inc(pT_dve, 1)

            def residual(w, g, t):
                if t == 0:
                    dve.wait_ge(xr_ready, g)
                dve.wait_ge(work_filled, w.count(("O", t)))
                if t >= 2:
                    dve.wait_ge(x2_stored[t % 2], (g - 1) * (16 * TPG // 2) + 16 * (t // 2))
                dve.scalar_tensor_tensor(out=x2[:, t % 2, :], in0=wbank(w.bank(("O", t))), scalar=tgx[:, 0:1],
                                         in1=xr[:, t, :], op0=ALU.mult, op1=ALU.add).then_inc(work_drained, 1)
                if t % 2:
                    dve.wait_ge(work_drained, w.count(("O", t)))
                    norm_stats(lambda u: x2[:, u % 2, :], t - 1, 2)
                    for u in (t - 1, t):
                        if u >= 2:
                            dve.wait_ge(xn2_stored[u % 2], (g - 1) * (16 * TPG // 2) + 16 * (u // 2))
                        normalise(xn2[:, u % 2, :], x2[:, u % 2, :], u).then_inc(xn2_ready, 1)

            def take_x2T(w, t):
                dve.wait_ge(work_filled, w.count(("x2T", t)))
                dve.tensor_copy(x2T[:, :, t * P:(t + 1) * P],
                                wbank(w.bank(("x2T", t))).rearrange("p (c n) -> p c n", c=DC))\
                    .then_inc(work_drained, 1)

            def choose(w, g):
                dve.wait_ge(work_filled, w.count(("lg", 0)))
                dve.tensor_tensor(logits[:], wbank(w.bank(("lg", 0)))[:, 0:TPG * E].rearrange(
                    "p (t e) -> p t e", t=TPG), rb_sb[:, None, :].broadcast_to([P, TPG, E]), ALU.add)\
                    .then_inc(work_drained, 1)
                wait_apart(dve, work_drained, w.count(("lg", 0)))
                for t in range(TPG):
                    ins = dve.max(top[:, t, :], logits[:, t, :])
                link(ins)
                dve.sem_inc(passed, 1)
                for t in range(TPG):
                    ins = dve.max_index(topi[:, t, :], top[:, t, :], logits[:, t, :])
                link(ins)
                dve.tensor_tensor(vdiff[:], top[:, :, 1], top[:, :, 0], ALU.subtract).then_inc(vdiff_ready, 1)
                link(dve.tensor_copy(topf[:], topi[:, :, 0:2].rearrange("p t k -> p k t")))
                for k in range(2):
                    ins = dve.tensor_tensor(onehot[:, k], iota_e[:, None, :].broadcast_to([P, TPG, E]),
                                            topf[:, k, :, None].broadcast_to([P, TPG, E]), ALU.is_equal)
                link(ins)
                dve.tensor_tensor(chosen[:], onehot[:, 0], onehot[:, 1], ALU.add).then_inc(chosen_ready, 1)

            def place(w, g):
                dve.wait_ge(work_filled, w.count(("rt", 0)))
                bank = wbank(w.bank(("rt", 0)))
                for t in range(TPG):
                    link(dve.tensor_tensor(run[:, t + 1, :], run[:, t, :],
                                           bank[:, (TPG + t) * E:(TPG + t + 1) * E], ALU.add))
                dve.tensor_tensor(pos[:], bank[:, 0:TPG * E].rearrange("p (t e) -> p t e", t=TPG),
                                  run[:, 0:TPG, :], ALU.add).then_inc(work_drained, 1)
                dve.wait_ge(work_drained, w.count(("rt", 0)))
                dve.tensor_copy(run[:, 0, :], run[:, TPG, :])
                for k in range(2):
                    ins = dve.tensor_tensor(prod[:, k], onehot[:, k], pos[:], ALU.mult)
                link(ins)
                link(dve.tensor_reduce(pk[:], prod[:], AX.X, ALU.add))
                dve.tensor_scalar(kept[:], pk[:], float(CAP), None, ALU.is_lt)
                link(dve.tensor_scalar(part[:], pk[:], float(P), None, ALU.is_ge))
                for m in range(2, ST):
                    link(dve.scalar_tensor_tensor(out=part[:], in0=pk[:], scalar=float(m * P), in1=part[:],
                                                  op0=ALU.is_ge, op1=ALU.add))
                link(dve.tensor_scalar(part[:], part[:], -float(P * ST - 1), None, ALU.mult))
                link(dve.scalar_tensor_tensor(out=dest_f[:], in0=pk[:], scalar=float(ST), in1=part[:],
                                              op0=ALU.mult, op1=ALU.add))
                link(dve.scalar_tensor_tensor(out=dest_f[:], in0=topf[:], scalar=float(CAP), in1=dest_f[:],
                                              op0=ALU.mult, op1=ALU.add))
                link(dve.tensor_tensor(dest_f[:], dest_f[:], trash_f[:], ALU.subtract))
                link(dve.tensor_tensor(dest_f[:], dest_f[:], kept[:], ALU.mult))
                link(dve.tensor_tensor(dest_f[:], dest_f[:], trash_f[:], ALU.add))
                dve.wait_ge(gexp_done, g)
                link(dve.tensor_scalar(den[:], gexp[:], 1.0, None, ALU.add))
                link(dve.reciprocal(gk[:, 0, :], den[:]))
                link(dve.tensor_tensor(gk[:, 1, :], gk[:, 0, :], gexp[:], ALU.mult))
                link(dve.tensor_tensor(gk[:], gk[:], kept[:], ALU.mult))
                link(dve.tensor_tensor(den[:], gk[:, 0, :], gk[:, 1, :], ALU.add))
                link(dve.tensor_scalar(den[:], den[:], 1e-9, None, ALU.add))
                link(dve.reciprocal(den[:], den[:]))
                for k in range(2):
                    ins = dve.tensor_tensor(gk[:, k, :], gk[:, k, :], den[:], ALU.mult)
                link(ins)
                dve.wait_ge(entry_free, g)
                dve.tensor_copy(dest[:], dest_f[:])
                for k in range(2):
                    dve.tensor_copy(entry[:, k, :, 0], tok_f[:])
                link(dve.tensor_scalar(entry[:, :, :, 1].bitcast(F32), gk[:], tgf[:, 0:1], None, ALU.mult))
                dve.tensor_scalar(tok_f[:], tok_f[:], float(GT), None, ALU.add)
                dve.tensor_scalar(trash_f[:], trash_f[:], float(GT), None, ALU.add).then_inc(entry_ready, 1)
                dve.wait_ge(entry_ready, g)

            def step(g, links):
                steps.enter(links)
                w = work_of(g)
                first, last, past = (isinstance(g, int) and g == v for v in (0, G - 1, G))
                more = not (last or past)
                if not past:
                    dve.tensor_scalar(v_cur[:], v_all[:, bass.ds((g // GPB) * D, D)], 1.0, None, ALU.mult)\
                        .then_inc(v_ready, 1)
                for j in range(NHALF):
                    if not past:
                        row_max(g, j)
                        if j >= 1:
                            softmax_norm(g, j - 1)
                        if j >= 2:
                            take_pT(g, j - 2)
                    for kind, t in SLOT_WORK[j]:
                        if kind == "O" and not first:
                            residual(w, g, t)
                        if kind == "x2T" and not first:
                            take_x2T(w, t)
                        if kind == "lg" and not first:
                            choose(w, g)
                        if kind == "xT" and more:
                            x_lo(w, g + 1, t)
                    if more:
                        if j == 3:
                            x_stats(g + 1)
                        if 3 <= j < 3 + TPG:
                            x_norm(j - 3)
                if not past:
                    softmax_norm(g, NHALF - 1)
                if more:
                    query_lo(w, g + 1, 0)
                    query_lo(w, g + 1, 1)
                if not past:
                    take_pT(g, NHALF - 2)
                if more:
                    query_lo(w, g + 1, 2)
                    query_lo(w, g + 1, 3)
                if not past:
                    take_pT(g, NHALF - 1)
                if not first:
                    place(w, g)
                if not past:
                    for c in range(DC):
                        dve.wait_ge(o_hi, DC * g + c + 1)
                        dve.tensor_tensor(oT_l[:, c, :], wbank(w.bank(("pv", c))), f32(oT_h[:, c, :]),
                                          ALU.subtract).then_inc(work_drained, 1)
                return steps.n

            w = work_of(-1)
            x_stats(0)
            for t in range(TPG):
                if t >= 2:
                    x_lo(w, 0, t - 2)
                x_norm(t)
            x_lo(w, 0, 2)
            x_lo(w, 0, 3)
            for c in range(DC):
                query_lo(w, 0, c)
            assert steps.n == LINKS_PROLOGUE, steps.n
            base = 2 + LINKS_PROLOGUE
            n = step(0, base)
            assert n == LINKS_FIRST, n
            base += LINKS_FIRST
            with dve.Fori(1, G - 1) as g:
                n = step(g, (g - 1) * LINKS_MID + base)
                assert n == LINKS_MID, n
            base += LINKS_MID * (G - 2)
            n = step(G - 1, base)
            assert n == LINKS_LAST, n
            base += n
            step(G, base)
            dve.drain().then_inc(phase1_done, 1)
            dve.wait_ge(phase1_done, 3)

            def weights_lo(u, e):
                r, n, k = (u // UPL) % NRAW, u % UPL, e * FU + u + 1
                dve.wait_ge(w1_hi, k)
                dve.tensor_tensor(w1_l[:, u % 4], raw1[:, r, n * D:(n + 1) * D].rearrange("p (c n) -> p c n", c=DC),
                                  f32(w1_h[:, u % 4]), ALU.subtract).then_inc(w1_split, 1)
                dve.wait_ge(w2_hi, k)
                dve.tensor_tensor(w2_l[:, u % 4], raw2[:, r, n * D:(n + 1) * D], f32(w2_h[:, u % 4]),
                                  ALU.subtract).then_inc(w2_split, 1)

            def rows_lo(e, i):
                dve.wait_ge(xg_hi, e * ST + i + 1)
                cols = slice(i * P, (i + 1) * P)
                dve.tensor_tensor(xT_l[:, :, cols], psum[:, 5 + i % 3, :].rearrange("p (c n) -> p c n", c=DC),
                                  f32(xT_h[:, :, cols]), ALU.subtract).then_inc(xg_split, 1)

            weights_lo(0, 0)
            weights_lo(1, 0)
            for i in range(ST):
                rows_lo(0, i)
            with dve.Fori(0, E) as e:
                dve.tensor_scalar(b1_cur[:], b1_sb[:, bass.ds(e * FU, FU)], 1.0, None, ALU.mult)\
                    .then_inc(b1_taken, 1)
                for u in range(FU):
                    weights_lo(u + 2, e)
                    for half in range(2):
                        cols = slice(half * CAP // 2, (half + 1) * CAP // 2)
                        dve.wait_ge(h_gelu, e * (2 * FU) + 2 * u + half + 1)
                        dve.tensor_tensor(h_l[:, u % 3, cols], h_f[:, u % 3, cols], f32(h_h[:, u % 3, cols]),
                                          ALU.subtract).then_inc(h_split, 1)
                for i in range(ST):
                    rows_lo(e + 1, i)
                dve.wait_ge(b2_loaded, 16 * e + 16)
                for i in range(ST):
                    dve.wait_ge(y_filled, e * ST + i + 1)
                    dve.tensor_tensor(y_sb[:, i, :], psum[:, i, :], b2_sb[:], ALU.add).then_inc(y_biased, 1)


def _cols(v):
    import numpy as np
    return np.ascontiguousarray(v.reshape(-1, P).T)


def kernel(x, ctx_1024, g_xattn, g_ffn, L0_xattn_w_q, L0_xattn_b_q, L0_xattn_w_k, L0_xattn_b_k, L0_xattn_w_v,
           L0_xattn_b_v, L0_xattn_w_o, L0_xattn_b_o, L0_ffn_router_w, L0_ffn_router_b, L0_ffn_w1, L0_ffn_b1,
           L0_ffn_w2, L0_ffn_b2):
    import numpy as np
    import concourse.bacc as bacc
    from concourse.bass_utils import run_bass_kernel_spmd

    def t(a):
        return np.ascontiguousarray(np.asarray(a).T)

    w1 = np.asarray(L0_ffn_w1).reshape(E, DC, P, PAIRS, UPL, P).transpose(0, 3, 2, 4, 1, 5)
    w2 = np.asarray(L0_ffn_w2).reshape(E, PAIRS, UPL, P, D).transpose(0, 1, 3, 2, 4)
    ins = [
        ("x", np.asarray(x).reshape(TOK, D)),
        ("ctxT", t(np.asarray(ctx_1024).reshape(BATCH * KEYS, D))),
        ("gx", np.asarray(g_xattn).reshape(1, 1)),
        ("gf", np.asarray(g_ffn).reshape(1, 1)),
        ("wqT", t(L0_xattn_w_q)), ("bq", _cols(np.asarray(L0_xattn_b_q))),
        ("wkT", t(L0_xattn_w_k)), ("bk", _cols(np.asarray(L0_xattn_b_k))),
        ("wvT", t(L0_xattn_w_v)), ("bv", np.asarray(L0_xattn_b_v).reshape(1, D)),
        ("woT", t(L0_xattn_w_o)), ("bo", np.asarray(L0_xattn_b_o).reshape(1, D)),
        ("rwT", t(L0_ffn_router_w)), ("rb", np.asarray(L0_ffn_router_b).reshape(1, E)),
        ("w1", np.ascontiguousarray(w1).reshape(E * PAIRS, P, UPL * D)),
        ("b1", _cols(np.asarray(L0_ffn_b1))),
        ("w2", np.ascontiguousarray(w2).reshape(E * PAIRS, P, UPL * D)),
        ("b2", np.asarray(L0_ffn_b2)),
    ]
    nc = bacc.Bacc("TRN2", target_bir_lowering=False, num_devices=1)
    arrays, args = {}, []
    for name, a in ins:
        a = np.ascontiguousarray(a)
        arrays["in_" + name] = a
        args.append(nc.dram_tensor("in_" + name, a.shape, mybir.dt.from_np(a.dtype), kind="ExternalInput").ap())
    args.append(nc.dram_tensor("out_rows", [TOK + CAP, D], F32, kind="ExternalOutput").ap())
    build(nc, *args)
    r = run_bass_kernel_spmd(nc, [arrays], core_ids=[0])
    return r.results[0]["out_rows"][:TOK].reshape(BATCH, SEQ, D)
```

```python
import concourse.bass as bass
from concourse import mybir
from contextlib import ExitStack

F32 = mybir.dt.float32
F32R = mybir.dt.float32r
I32 = mybir.dt.int32
U32 = mybir.dt.uint32
ALU = mybir.AluOpType
ACT = mybir.ActivationFunctionType
AX = mybir.AxisListType

P = 128
D = 512
DC = D // P
H = 16
DH = D // H
HQ = P // DH
KEYS = 128
BATCH = 2
SEQ = 2048
TOK = BATCH * SEQ
GT = 512
TPG = GT // P
G = TOK // GT
GPB = SEQ // GT
NHALF = 2 * TPG
HH = H // 2
SCALE = DH ** -0.5
EPS = 1e-5

E = 16
F = 2048
FU = F // P
CAP = -(-5 * TOK * 2 // (4 * E))
ST = CAP // P
UPL = 2
PAIRS = FU // UPL
NRAW = 4
TABLE = (E + 1) * CAP
assert CAP % P == 0
LEAST = 2

SLOTS = [
    [("x2T", 2, 2), ("q", 2, 0), ("x2T", 3, 2), ("pv", 0, 1)],
    [("q", 3, 0), ("pv", 1, 1), ("lg", 0, 2)],
    [("pv", 2, 1), ("pv", 3, 1)],
    [("O", 0, 1), ("xT", 0, -1), ("rt", 0, 2)],
    [("O", 1, 1), ("xT", 1, -1)],
    [("O", 2, 1), ("xT", 2, -1)],
    [("x2T", 0, 1), ("O", 3, 1), ("x2T", 1, 1), ("xT", 3, -1)],
    [("q", 0, -1), ("q", 1, -1)],
]
SIDE = [
    [["x stats 0"], ["x stats 1"], [], ["x stats 2"], [], ["x stats 3"]],
    [["x mean"], ["x seed"], ["c 0"], ["c 1"], ["c 2"]],
    [["x root 0"], ["x root 1"], ["x root 2"], ["x norm 0"]],
    [["p stats 0", "v"], [], ["t 0"], ["t 1"], ["x norm 1", "t 2"]],
    [["p stats 1", "p mean"], ["p seed"], ["p root 0"], ["x norm 2", "p root 1", "t 3"]],
    [["r stats 2"], ["p root 2"], ["t 4"], ["p norm 0", "p norm 1", "x norm 3"]],
    [[], ["r stats 3"], ["r mean"], ["r seed"], ["r root 0"], ["r root 1"]],
    [["r root 2"], ["r norm 2"], ["r norm 3"], []],
]
PREP_USES = 6
ITERATIONS = G + 2
LOOP = (2, G - 1)


def uses_of(g):
    def there(u):
        return not isinstance(g, int) or 0 <= g - u[2] < G
    return [u for slot in SLOTS for u in slot if there(u)]


ALL_USES = sum(len(slot) for slot in SLOTS)
LOOP_BASE = PREP_USES + sum(len(uses_of(g)) for g in range(-1, LOOP[0]))


class Work:

    def __init__(self, g):
        self.order = [u[:2] for u in uses_of(g)]
        if isinstance(g, int):
            self.base = PREP_USES + sum(len(uses_of(i)) for i in range(-1, g))
            self.parity = self.base % 2
        else:
            self.base = (g - LOOP[0]) * ALL_USES + LOOP_BASE
            self.parity = LOOP_BASE % 2
        self.g = g

    def has(self, lag):
        return not isinstance(self.g, int) or 0 <= self.g - lag < G

    def bank(self, *use):
        return (self.parity + self.order.index(use)) % 2

    def count(self, *use):
        return self.base + self.order.index(use) + 1

    def count_before(self, *use):
        if isinstance(self.g, int):
            return Work(self.g - 1).count(*use)
        return self.count(*use) - ALL_USES

    def slot(self, j):
        return [u for u in SLOTS[j] if self.has(u[2])]


class Steps:

    def __init__(self, eng, sem):
        self.eng, self.sem, self.base, self.n = eng, sem, 0, 0

    def mark(self, ins):
        self.n += 1
        ins.then_inc(self.sem, 1)

    def wait(self):
        self.eng.wait_ge(self.sem, self.base + self.n)

    def link(self, ins):
        self.mark(ins)
        self.wait()

    def enter(self, base):
        self.base, self.n = base, 0


LINKS_PREP = 2
LINKS_NORM = 13
LINKS_CHOOSE = 4
LINKS_PLACE = 23


def links_of(g):
    def has(lag):
        return not isinstance(g, int) or 0 <= g - lag < G
    return (has(0) * NHALF + has(-1) * (TPG + LINKS_NORM) + has(1) * (TPG + 2 * LINKS_NORM)
            + has(2) * (LINKS_CHOOSE + LINKS_PLACE))


def build(nc, x, ctxT, gx, gf, wqT, bq, wkT, bk, wvT, bv, woT, bo, rwT, rb, w1, b1, w2, b2, out):
    xn_dram = nc.dram_tensor("xn_rows", [TOK + CAP, D], F32, kind="Internal").ap()
    table = nc.dram_tensor("slot_table", [TABLE + 2 * TOK, 2], I32, kind="Internal").ap()

    ctx = ExitStack()
    with ctx:
        def sem(name):
            return ctx.enter_context(nc.semaphore(name))

        psum = ctx.enter_context(nc.psum_tensor("banks", [P, 8, 512], F32))

        def wbank(b):
            return psum[:, 4 + b, :]

        ident = ctx.enter_context(nc.sbuf_tensor("ident", [P, P], F32))
        tgx = ctx.enter_context(nc.sbuf_tensor("tanh_gx", [P, 1], F32))
        tgf = ctx.enter_context(nc.sbuf_tensor("tanh_gf", [P, 1], F32))
        n_tiles = ctx.enter_context(nc.sbuf_tensor("n_tiles", [P, E], I32))
        b1_sb = ctx.enter_context(nc.sbuf_tensor("b1_cols", [P, E * FU], F32))

        with ExitStack() as one:
            def sb(name, shape, dt=F32):
                return one.enter_context(nc.sbuf_tensor(name, shape, dt))

            kbd_h = sb("kbd_h", [P, BATCH * DC * HQ * KEYS], F32R)
            kbd_l = sb("kbd_l", [P, BATCH * DC * HQ * KEYS], F32R)
            before = sb("strict_upper", [P, P])
            ones = sb("ones", [P, P])
            iota_e = sb("iota_e", [P, E])
            iota_i = sb("iota_i", [P, E], I32)
            tok_i = sb("tok_i", [P, TPG], I32)
            trash_i = sb("trash_i", [P, 2, TPG], I32)
            tok_f = sb("tok_f", [P, TPG])
            trash_f = sb("trash_f", [P, 2, TPG])
            gates_in = sb("gates_in", [P, 2])
            bq_sb = sb("bq_sb", [P, DC])
            bk_sb = sb("bk_sb", [P, DC])
            bv_sb = sb("bv_sb", [P, D])
            bo_sb = sb("bo_sb", [P, D])
            rb_sb = sb("rb_sb", [P, E])
            rw_sb = sb("rw_sb", [P, DC, E])
            wq_h = sb("wq_h", [P, DC, D], F32R)
            wq_l = sb("wq_l", [P, DC, D], F32R)
            wo_h = sb("wo_h", [P, DC, D], F32R)
            wo_l = sb("wo_l", [P, DC, D], F32R)
            v_all = sb("v_all", [P, BATCH * D])
            v_cur = sb("v_cur", [P, D])
            x_sb = sb("x_sb", [P, TPG, D])
            xr = sb("xr", [P, TPG, D])
            xn = sb("xn", [P, 2, D])
            xnT_h = sb("xnT_h", [P, DC, GT], F32R)
            xnT_l = sb("xnT_l", [P, DC, GT], F32R)
            qT_h = sb("qT_h", [P, DC, GT], F32R)
            qT_l = sb("qT_l", [P, DC, GT], F32R)
            prob = sb("prob", [P, 2, HH, KEYS])
            probT = sb("probT", [P, H, GT])
            oT_h = sb("oT_h", [P, DC, GT], F32R)
            oT_l = sb("oT_l", [P, DC, GT], F32R)
            x2 = sb("x2", [P, 3, D])
            xn2 = sb("xn2", [P, 2, D])
            x2T = sb("x2T", [P, DC, GT])
            stats = sb("stats", [P, TPG, 6])
            x_mv = sb("x_mean_var", [P, TPG, 2]), sb("x_rstd", [P, TPG])
            pair_mv = sb("x2_mean_var", [P, TPG, 2]), sb("x2_rstd", [P, TPG])
            ve = sb("ve", [P, TPG])
            nhv = sb("neg_half_var", [P, TPG])
            nt = sb("newton", [P, TPG])
            nmax = sb("nmax", [P, 2, HH])
            nbias = sb("nbias", [P, 2, HH])
            psums = sb("prob_sums", [P, 2, HH])
            rinv = sb("rinv", [P, 2, HH])
            logits = sb("logits", [P, TPG, E])
            top = sb("top", [P, TPG, 8])
            topi = sb("topi", [P, TPG, 8], U32)
            topf = sb("topf", [P, 2, TPG])
            onehot = sb("onehot", [P, 2, TPG, E])
            chosen = sb("chosen", [P, TPG, E])
            run = sb("running_base", [P, TPG + 1, E])
            counts = sb("counts", [P, 2, TPG, E])
            pos = sb("pos", [P, TPG, E])
            prod = sb("prod", [P, 2, TPG, E])
            pk = sb("pk", [P, 2, TPG])
            kept = sb("kept", [P, 2, TPG])
            offs = sb("offs", [P, 2, TPG])
            dest_f = sb("dest_f", [P, 2, TPG])
            dest = sb("dest", [P, 2, TPG], I32)
            entry = sb("entry", [P, 2, TPG, 2], I32)
            vdiff = sb("vdiff", [P, TPG])
            gexp = sb("gexp", [P, TPG])
            gk = sb("gk", [P, 2, TPG])
            den = sb("den", [P, TPG])

        raw_w = [probT[:, 4 * i:4 * i + 4, :] for i in range(4)]
        ctx_sb = x2T[:, :, 0:BATCH * KEYS]
        fill = prob[:, :, :, :].rearrange("p a h k -> p (a h k)").bitcast(I32)

        with ExitStack() as two:
            def sb(name, shape, dt=F32):
                return two.enter_context(nc.sbuf_tensor(name, shape, dt))

            raw1 = sb("raw_w1", [P, NRAW, UPL * D])
            raw2 = sb("raw_w2", [P, NRAW, UPL * D])
            w1_h = sb("w1_h", [P, 4, DC, P], F32R)
            w1_l = sb("w1_l", [P, 4, DC, P], F32R)
            w2_h = sb("w2_h", [P, 4, D], F32R)
            w2_l = sb("w2_l", [P, 4, D], F32R)
            xg = sb("xg", [P, ST, D])
            xT_h = sb("xT_h", [P, DC, CAP], F32R)
            xT_l = sb("xT_l", [P, DC, CAP], F32R)
            h_f = sb("h_f", [P, 3, CAP])
            h_h = sb("h_h", [P, 3, CAP], F32R)
            h_l = sb("h_l", [P, 3, CAP], F32R)
            y_sb = sb("y_sb", [P, ST, D])
            y_w = sb("y_w", [P, ST, D])
            b2_sb = sb("b2_sb", [P, D])
            b1_cur = sb("b1_cur", [P, FU])
            tab_next = sb("tab_next", [P, ST, 2], I32)
            tab_cur = sb("tab_cur", [P, ST, 2], I32)

        const_done = sem("const_done")
        w_loaded = sem("w_loaded")
        small_loaded = sem("small_loaded")
        w_hi = sem("w_hi")
        kbd_ready = sem("kbd_ready")
        bo_ready = sem("bo_ready")
        tanh_done = sem("tanh_done")
        fill_ready = sem("fill_ready")
        init_stored = sem("init_stored")
        x_loaded = sem("x_loaded")
        xr_loaded = sem("xr_loaded")
        xr_ready = sem("xr_ready")
        dve_step = sem("dve_step")
        xn_ready = sem("xn_ready")
        work_filled = sem("work_filled")
        work_drained = sem("work_drained")
        xT_hi = sem("xT_hi")
        q_hi = sem("q_hi")
        o_hi = sem("o_hi")
        s_filled = sem("s_filled")
        nbias_ready = sem("nbias_ready")
        exp_done = sem("exp_done")
        prob_ready = sem("prob_ready")
        pT_filled = sem("pT_filled")
        pT_taken = sem("pT_taken")
        rinv_ready = sem("rinv_ready")
        v_ready = sem("v_ready")
        xn2_ready = sem("xn2_ready")
        x2_stored = [sem(f"x2_stored{i}") for i in range(2)]
        xn2_stored = [sem(f"xn2_stored{i}") for i in range(2)]
        chosen_ready = sem("chosen_ready")
        vdiff_ready = sem("vdiff_ready")
        gexp_done = sem("gexp_done")
        entry_ready = sem("entry_ready")
        scattered = sem("scattered")
        entry_free = sem("entry_free")
        phase1_done = sem("phase1_done")

        raw_loaded = [sem(f"raw_loaded{i}") for i in range(NRAW)]
        w1_hi = sem("w1_hi")
        w1_split = sem("w1_split")
        w2_hi = sem("w2_hi")
        w2_split = sem("w2_split")
        tab_loaded = sem("tab_loaded")
        tab_taken = sem("tab_taken")
        gathered = [sem(f"gathered{i}") for i in range(ST)]
        xg_turned = sem("xg_turned")
        xg_hi = sem("xg_hi")
        xg_split = sem("xg_split")
        h_filled = sem("h_filled")
        h_gelu = sem("h_gelu")
        h_split = sem("h_split")
        down_done = sem("down_done")
        y_filled = sem("y_filled")
        y_biased = sem("y_biased")
        y_weighted = sem("y_weighted")
        b2_loaded = sem("b2_loaded")
        added = sem("added")
        passed = sem("passed")
        b1_taken = sem("b1_taken")

        def wait_apart(eng, s, value):
            eng.wait_ge(s, value)
            eng.sem_inc(passed, 1)

        def first_wait(eng, s, value):
            if not isinstance(value, int) or value > 0:
                eng.wait_ge(s, value)

        def parts_of(n):
            if n * P <= 512:
                return [(slice(0, n * P), 2)]
            return [(slice(0, CAP // 2), 1), (slice(CAP // 2, CAP), 1)]

        def h_bank(n, u, part):
            return psum[:, 5 + (len(parts_of(n)) * u + part) % 3, :]

        def tile_count(n, i):
            return 1 if i < n - 1 else 1 + ST - n

        def by_tiles(eng, e, body):
            found = eng.value_load(n_tiles[0:1, bass.ds(e, 1)], min_val=LEAST, max_val=ST)
            for n in range(LEAST, ST + 1):
                with eng.If(found == n):
                    body(n)

        def rows_of(t, g):
            return t[bass.ds(g * GT, GT), :].rearrange("(t p) n -> p t n", p=P)

        block = ctx.enter_context(nc.Block())

        @block.sync
        def _(sp):
            sp.dma_start(ctx_sb, ctxT.rearrange("(c p) n -> p c n", p=P)).then_inc(w_loaded, 16)
            for i, w in enumerate((wqT, wkT, wvT, woT)):
                sp.dma_start(raw_w[i], w.rearrange("(c p) n -> p c n", p=P)).then_inc(w_loaded, 16)
            sp.dma_start(x_sb[:], rows_of(x, 0)).then_inc(x_loaded, 16)
            sp.dma_start(rw_sb[:], rwT.rearrange("(c p) n -> p c n", p=P)).then_inc(small_loaded, 16)
            sp.dma_start(bq_sb[:], bq).then_inc(small_loaded, 16)
            sp.dma_start(bk_sb[:], bk).then_inc(small_loaded, 16)
            for dst, src in ((bv_sb[:], bv), (bo_sb[:], bo), (rb_sb[:], rb),
                             (gates_in[:, 0:1], gx), (gates_in[:, 1:2], gf)):
                sp.dma_start(dst, src.broadcast_to(list(dst.shape))).then_inc(small_loaded, 16)
            sp.dma_start(b1_sb[:], b1).then_inc(small_loaded, 16)
            sp.dma_start(xr[:], rows_of(x, 0)).then_inc(xr_loaded, 16)
            sp.wait_ge(fill_ready, 2)
            sp.dma_start(table[0:TABLE, :].rearrange("(e s) w -> e (s w)", s=CAP),
                         fill[0:E + 1, 0:2 * CAP]).then_inc(init_stored, 16)
            for i in range(ST):
                rows = slice(TOK + i * P, TOK + (i + 1) * P)
                sp.dma_start(xn_dram[rows, :], x2[:, 0, :]).then_inc(init_stored, 16)
                sp.dma_start(out[rows, :], x2[:, 0, :]).then_inc(init_stored, 16)

            def load_x(g):
                sp.wait_ge(xn_ready, TPG * g)
                sp.dma_start(x_sb[:], rows_of(x, g)).then_inc(x_loaded, 16)

            def store_x2(w, g, t):
                sp.wait_ge(work_drained, w.count("O", t))
                sp.dma_start(out[bass.ds(g * GT + t * P, P), :], x2[:, t % 3, :])\
                    .then_inc(x2_stored[min(t % 3, 1)], 16)

            def store_xn2(g, t):
                sp.wait_ge(xn2_ready, g * TPG + t + 1)
                sp.dma_start(xn_dram[bass.ds(g * GT + t * P, P), :], xn2[:, t % 2, :])\
                    .then_inc(xn2_stored[t % 2], 16)

            def loads_and_stores(g):
                w = Work(g)
                if w.has(1):
                    for t in range(3):
                        store_x2(w, g - 1, t)
                    for t in range(2):
                        store_xn2(g - 1, t)
                if w.has(-2):
                    load_x(g + 2)
                if w.has(1):
                    store_x2(w, g - 1, 3)
                    for t in range(2, TPG):
                        store_xn2(g - 1, t)
                    for i in range(2):
                        sp.wait_ge(x2_stored[i], g * (16 * TPG // 2))
                        sp.wait_ge(xn2_stored[i], g * (16 * TPG // 2))
                    if w.has(0):
                        sp.dma_start(xr[:], rows_of(x, g)).then_inc(xr_loaded, 16)

            load_x(1)
            for g in range(LOOP[0]):
                loads_and_stores(g)
            with sp.Fori(LOOP[0], G - 2) as g:
                loads_and_stores(g)
            for g in range(G - 2, G + 1):
                loads_and_stores(g)

            sp.wait_ge(s_filled, NHALF * G)

            def load_weights(e, pair, turn):
                r = pair % NRAW
                if turn is not None:
                    sp.wait_ge(w1_split, turn)
                    sp.wait_ge(w2_split, turn)
                src = bass.ds(e * PAIRS + pair, 1)
                sp.dma_start(raw1[:, r, :], w1[src].rearrange("a p n -> p (a n)")).then_inc(raw_loaded[r], 16)
                sp.dma_start(raw2[:, r, :], w2[src].rearrange("a p n -> p (a n)")).then_inc(raw_loaded[r], 16)

            for pair in range(NRAW):
                load_weights(0, pair, None)
            with sp.Fori(0, E - 1) as e:
                for pair in range(PAIRS):
                    ahead = pair + NRAW
                    load_weights(e + ahead // PAIRS, ahead % PAIRS, e * FU + UPL * (pair + 1))
                    if pair == NRAW:
                        sp.dma_start(b2_sb[:], b2[bass.ds(e, 1), :].broadcast_to([P, D])).then_inc(b2_loaded, 16)
            for pair in range(PAIRS - NRAW):
                load_weights(E - 1, pair + NRAW, (E - 1) * FU + UPL * (pair + 1))
            load_weights(E - 1, 0, (E - 1) * FU + UPL * (PAIRS - NRAW + 1))
            sp.dma_start(b2_sb[:], b2[E - 1:E, :].broadcast_to([P, D])).then_inc(b2_loaded, 16)

        @block.gpsimd
        def _(pool):
            pool.memset(ident[:], 0.0).then_inc(const_done, 1)
            pool.memset(before[:], 0.0).then_inc(const_done, 1)
            pool.memset(ones[:], 1.0).then_inc(const_done, 1)
            pool.wait_ge(const_done, 3)
            pool.affine_select(out=ident[:], in_=ident[:], compare_op=ALU.not_equal, fill=1.0, base=0,
                               pattern=[[-1, P]], channel_multiplier=1).then_inc(const_done, 1)
            pool.affine_select(out=before[:], in_=before[:], compare_op=ALU.is_ge, fill=1.0, base=0,
                               pattern=[[-1, P]], channel_multiplier=1).then_inc(const_done, 1)
            pool.iota(iota_i[:], pattern=[[1, E]], base=0, channel_multiplier=0).then_inc(const_done, 1)
            pool.iota(tok_i[:], pattern=[[P, TPG]], base=0, channel_multiplier=1).then_inc(const_done, 1)
            pool.iota(trash_i[:], pattern=[[TOK, 2], [P, TPG]], base=TABLE, channel_multiplier=1)\
                .then_inc(const_done, 1)
            pool.memset(x2[:, 0, :], 0.0).then_inc(fill_ready, 1)
            pool.memset(fill[0:E + 1, 0:2 * CAP], 0).then_inc(const_done, 1)
            pool.wait_ge(const_done, 9)
            pool.iota(fill[0:E + 1, 0:2 * CAP:2], pattern=[[1, CAP]], base=TOK, channel_multiplier=0)\
                .then_inc(fill_ready, 1)

            def add_bo(g):
                pool.wait_ge(xr_loaded, 16 * g + 16)
                pool.tensor_tensor(xr[:], xr[:], bo_sb[:, None, :].broadcast_to([P, TPG, D]), ALU.add)\
                    .then_inc(xr_ready, 1)

            def scatter(g, t):
                wait_apart(pool, entry_ready, g + 1)
                for k in range(2):
                    pool.indirect_dma_start(
                        out=table[:, :], out_offset=bass.IndirectOffsetOnAxis(ap=dest[:, k, t:t + 1], axis=0),
                        in_=entry[:, k, t, :], in_offset=None).then_inc(scattered, 16)

            def softmax_norm(g, j):
                pool.wait_ge(rinv_ready, NHALF * g + j + 1)
                pool.tensor_tensor(prob[:, j % 2], prob[:, j % 2],
                                   rinv[:, j % 2, :, None].broadcast_to([P, HH, KEYS]), ALU.mult)\
                    .then_inc(prob_ready, 1)

            def step(g):
                w = Work(g)
                for j in range(NHALF):
                    if j >= 1 and w.has(0):
                        softmax_norm(g, j - 1)
                    if j == 0 and w.has(1):
                        softmax_norm(g - 1, NHALF - 1)
                        add_bo(g - 1)
                    if j >= TPG and w.has(2):
                        scatter(g - 2, j - TPG)
                if w.has(2):
                    pool.wait_ge(scattered, (g - 1) * (16 * 2 * TPG))
                    pool.sem_inc(entry_free, 1)

            pool.wait_ge(bo_ready, 1)
            pool.wait_ge(init_stored, 16 * (1 + 2 * ST))
            pool.sem_inc(entry_free, 1)
            for g in range(LOOP[0]):
                step(g)
            with pool.Fori(*LOOP) as g:
                step(g)
            for g in range(LOOP[1], ITERATIONS):
                step(g)
            pool.wait_ge(phase1_done, 3)
            for i in range(2):
                pool.wait_ge(x2_stored[i], 16 * TPG // 2 * G)
                pool.wait_ge(xn2_stored[i], 16 * TPG // 2 * G)

            def load_table(e):
                pool.dma_start(tab_next[:], table[bass.ds(e * CAP, CAP), :].rearrange("(p i) w -> p i w", i=ST))\
                    .then_inc(tab_loaded, 16)

            def gather(e):
                wait_apart(pool, tab_loaded, 16 * e + 16)
                for i in range(ST):
                    pool.indirect_dma_start(
                        out=xg[:, i, :], out_offset=None, in_=xn_dram[:, :],
                        in_offset=bass.IndirectOffsetOnAxis(ap=tab_next[:, i, 0:1], axis=0))\
                        .then_inc(gathered[i], 16)

            additions = pool.alloc_register("additions")
            pool.reg_mov(additions, 0)
            load_table(0)
            gather(0)
            with pool.Fori(0, E) as e:
                pool.tensor_copy(tab_cur[:], tab_next[:]).then_inc(tab_taken, 1)
                pool.wait_ge(tab_taken, e + 1)
                for i in range(ST):
                    pool.wait_ge(gathered[i], 16 * e + 16)
                load_table(e + 1)
                pool.wait_ge(xg_turned, ST * (e + 1))
                gather(e + 1)

                def add_rows(n):
                    for i in range(n):
                        wait_apart(pool, y_weighted, e * ST + i + 1)
                        pool.indirect_dma_start(
                            out=out[:, :], out_offset=bass.IndirectOffsetOnAxis(ap=tab_cur[:, i, 0:1], axis=0),
                            in_=y_w[:, i, :], in_offset=None, compute_op=ALU.add).then_inc(added, 16)
                        pool.reg_add(additions, additions, 16)
                        pool.wait_ge(added, additions)

                by_tiles(pool, e, add_rows)
            for i in range(ST):
                pool.wait_ge(gathered[i], 16 * (E + 1))

        @block.scalar
        def _(act):
            act.wait_ge(small_loaded, 16 * 9)
            act.activation(tgx[:], gates_in[:, 0:1], ACT.Tanh).then_inc(tanh_done, 1)
            act.activation(tgf[:], gates_in[:, 1:2], ACT.Tanh).then_inc(tanh_done, 1)
            act.wait_ge(w_loaded, 16 * 5)
            for c in range(DC):
                act.wait_ge(work_filled, c + 1)
                act.activation(xnT_h[:, c, 0:BATCH * KEYS], wbank(c % 2)[:, 0:BATCH * KEYS], ACT.Identity,
                               bias=bk_sb[:, c:c + 1]).then_inc(w_hi, 1)
            act.activation(wq_h[:], raw_w[0], ACT.Copy).then_inc(w_hi, 1)
            act.activation(wo_h[:], raw_w[3], ACT.Copy).then_inc(w_hi, 1)
            act.wait_ge(kbd_ready, 1)

            def x_hi(w, t):
                act.wait_ge(work_filled, w.count("xT", t))
                act.activation(xnT_h[:, :, t * P:(t + 1) * P],
                               wbank(w.bank("xT", t)).rearrange("p (c n) -> p c n", c=DC), ACT.Copy)\
                    .then_inc(xT_hi, 1)

            def query_hi(w, c):
                act.wait_ge(work_filled, w.count("q", c))
                act.activation(qT_h[:, c, :], wbank(w.bank("q", c)), ACT.Identity,
                               bias=bq_sb[:, c:c + 1]).then_inc(q_hi, 1)

            def exps(g, j):
                act.wait_ge(nbias_ready, NHALF * g + j + 1)
                first_wait(act, pT_filled, NHALF * g + j - 1)
                for h in range(HH):
                    ins = act.activation(prob[:, j % 2, h, :],
                                         psum[:, 2 * (j % 2) + h // HQ, (h % HQ) * KEYS:(h % HQ + 1) * KEYS],
                                         ACT.Exp, bias=nbias[:, j % 2, h:h + 1], scale=SCALE,
                                         accum_out=psums[:, j % 2, h:h + 1])
                ins.then_inc(exp_done, 1)

            def take_pT(g, j):
                act.wait_ge(pT_filled, NHALF * g + j + 1)
                h0, t = (j // TPG) * HH, j % TPG
                act.activation(probT[:, h0:h0 + HH, t * P:(t + 1) * P],
                               psum[:, 6:8, :].rearrange("p a (h n) -> p (a h) n", h=HQ), ACT.Copy)\
                    .then_inc(pT_taken, 1)

            def step(g):
                w = Work(g)
                for j in range(NHALF):
                    for kind, i, _ in w.slot(j):
                        if kind == "xT":
                            x_hi(w, i)
                        elif kind == "q":
                            query_hi(w, i)
                        elif kind == "pv":
                            act.wait_ge(work_filled, w.count("pv", i))
                            act.activation(oT_h[:, i, :], wbank(w.bank("pv", i)), ACT.Copy).then_inc(o_hi, 1)
                        elif kind == "rt":
                            act.wait_ge(vdiff_ready, g - 1)
                            act.activation(gexp[:], vdiff[:], ACT.Exp).then_inc(gexp_done, 1)
                    if j < 2 and w.has(1):
                        take_pT(g - 1, NHALF - 2 + j)
                    if j >= 2 and w.has(0):
                        take_pT(g, j - 2)
                    if w.has(0):
                        exps(g, j)

            w = Work(-1)
            for t in range(TPG):
                x_hi(w, t)
            for c in range(2):
                query_hi(w, c)
            act.wait_ge(init_stored, 16 * (1 + 2 * ST))
            for g in range(LOOP[0]):
                step(g)
            with act.Fori(*LOOP) as g:
                step(g)
            for g in range(LOOP[1], ITERATIONS):
                step(g)
            act.drain().then_inc(phase1_done, 1)
            act.wait_ge(phase1_done, 3)

            def weights_hi(u, e):
                pair, r = (u // UPL) % PAIRS, (u // UPL) % NRAW
                n = u % UPL
                act.wait_ge(raw_loaded[r], e * (32 * PAIRS // NRAW) + 32 * ((u // UPL) // NRAW + 1))
                act.activation(w1_h[:, u % 4], raw1[:, r, n * D:(n + 1) * D].rearrange("p (c n) -> p c n", c=DC),
                               ACT.Copy).then_inc(w1_hi, 1)
                if u >= 4:
                    act.wait_ge(down_done, e * (FU - 1) + u - 3)
                act.activation(w2_h[:, u % 4], raw2[:, r, n * D:(n + 1) * D], ACT.Copy).then_inc(w2_hi, 1)

            def rows_hi(e, i):
                act.wait_ge(xg_turned, e * ST + i + 1)
                act.activation(xT_h[:, :, i * P:(i + 1) * P],
                               psum[:, 5 + i % 3, :].rearrange("p (c n) -> p c n", c=DC), ACT.Copy)\
                    .then_inc(xg_hi, 1)

            weights_hi(0, 0)
            weights_hi(1, 0)
            for i in range(ST):
                rows_hi(0, i)
            def expert(e, n):
                for u in range(FU):
                    weights_hi(u + 2, e)
                    for part, (cols, counts_for) in enumerate(parts_of(n)):
                        act.wait_ge(h_filled, e * (2 * FU) + 2 * u + part + counts_for)
                        hp = h_bank(n, u, part)[:, 0:cols.stop - cols.start]
                        bias = b1_cur[:, u:u + 1]
                        act.activation(h_f[:, u % 3, cols], hp, ACT.Gelu, bias=bias)
                        act.activation(h_h[:, u % 3, cols], hp, ACT.Gelu, bias=bias).then_inc(h_gelu, counts_for)
                for i in range(ST):
                    rows_hi(e + 1, i)
                act.wait_ge(tab_taken, e + 1)
                for i in range(n):
                    act.wait_ge(y_biased, e * ST + i + 1)
                    act.activation(y_w[:, i, :], y_sb[:, i, :], ACT.Copy,
                                   scale=tab_cur[:, i, 1:2].bitcast(F32)).then_inc(y_weighted, tile_count(n, i))

            with act.Fori(0, E) as e:
                act.wait_ge(b1_taken, e + 1)
                by_tiles(act, e, lambda n: expert(e, n))

        @block.tensor
        def _(pe):
            def product(dst, pairs, cols=None):
                n = len(pairs)
                for i, (ah, al, bh, bl) in enumerate(pairs):
                    pe.matmul(dst, ah, bh, start=(i == 0), stop=False)
                    pe.matmul(dst, ah, bl, start=False, stop=False)
                    ins = pe.matmul(dst, al, bh, start=False, stop=(i == n - 1))
                return ins

            def take(w, use):
                pe.wait_ge(work_drained, w.count(*use) - 2)
                return wbank(w.bank(*use))

            pe.wait_ge(w_loaded, 16 * 5)
            for c in range(DC):
                if c >= 2:
                    pe.wait_ge(work_drained, c - 1)
                for i in range(DC):
                    ins = pe.matmul(wbank(c % 2)[:, 0:BATCH * KEYS], raw_w[1][:, i, c * P:(c + 1) * P],
                                    ctx_sb[:, i, :], start=(i == 0), stop=(i == DC - 1))
                ins.then_inc(work_filled, 1)
            for b in range(BATCH):
                pe.wait_ge(work_drained, DC + b - 1)
                for i in range(DC):
                    ins = pe.matmul(wbank(b), ctx_sb[:, i, b * KEYS:(b + 1) * KEYS], raw_w[2][:, i, :],
                                    start=(i == 0), stop=(i == DC - 1))
                ins.then_inc(work_filled, 1)
            pe.wait_ge(const_done, 9)

            def turn_x(w, g, t):
                pe.wait_ge(xn_ready, TPG * g + t + 1)
                dst = take(w, ("xT", t))
                for c in range(DC):
                    ins = pe.transpose(dst[:, c * P:(c + 1) * P], xn[:, t % 2, c * P:(c + 1) * P], ident[:])
                ins.then_inc(work_filled, 1)

            def query(w, c):
                if c == 0:
                    pe.wait_ge(work_drained, w.count("xT", TPG - 1))
                dst = take(w, ("q", c))
                cs = slice(c * P, (c + 1) * P)
                product(dst, [(wq_h[:, i, cs], wq_l[:, i, cs], xnT_h[:, i, :], xnT_l[:, i, :])
                              for i in range(DC)]).then_inc(work_filled, 1)

            def scores(w, g, j):
                if j == 0:
                    pe.wait_ge(work_drained, w.count_before("q", 1))
                if j == TPG:
                    pe.wait_ge(work_drained, w.count("q", 3))
                first_wait(pe, exp_done, NHALF * g + j - 1)
                t = j % TPG
                ts = slice(t * P, (t + 1) * P)
                for n in range(2):
                    c = 2 * (j // TPG) + n
                    off = (g // GPB) * (DC * HQ * KEYS) + c * HQ * KEYS
                    kh, kl = (k[:, bass.ds(off, HQ * KEYS)] for k in (kbd_h, kbd_l))
                    ins = product(psum[:, 2 * (j % 2) + n, :], [(qT_h[:, c, ts], qT_l[:, c, ts], kh, kl)])
                ins.then_inc(s_filled, 1)

            def turn_probs(g, j):
                pe.wait_ge(prob_ready, NHALF * g + j + 1)
                first_wait(pe, pT_taken, NHALF * g + j)
                for h in range(HH):
                    ins = pe.transpose(psum[:, 6 + h // HQ, (h % HQ) * P:(h % HQ + 1) * P],
                                       prob[:, j % 2, h, :], ident[:])
                ins.then_inc(pT_filled, 1)

            def context(w, g, c):
                if c % 2 == 0:
                    pe.wait_ge(pT_taken, NHALF * g + TPG * (c // 2 + 1))
                if c == 0:
                    pe.wait_ge(v_ready, g + 1)
                dst = take(w, ("pv", c))
                for n in range(HQ):
                    h = HQ * c + n
                    ins = pe.matmul(dst[n * DH:(n + 1) * DH, :], v_cur[:, h * DH:(h + 1) * DH], probT[:, h, :],
                                    start=True, stop=True)
                ins.then_inc(work_filled, 1)

            def project(w, t):
                if t == 0:
                    pe.wait_ge(work_drained, w.count("pv", DC - 1))
                dst = take(w, ("O", t))
                ts = slice(t * P, (t + 1) * P)
                product(dst, [(oT_h[:, c, ts], oT_l[:, c, ts], wo_h[:, c, :], wo_l[:, c, :])
                              for c in range(DC)]).then_inc(work_filled, 1)

            def turn_x2(w, g, t):
                pe.wait_ge(xn2_ready, TPG * g + t + 1)
                dst = take(w, ("x2T", t))
                for c in range(DC):
                    ins = pe.transpose(dst[:, c * P:(c + 1) * P], xn2[:, t % 2, c * P:(c + 1) * P], ident[:])
                ins.then_inc(work_filled, 1)

            def route_logits(w):
                pe.wait_ge(work_drained, w.count("x2T", TPG - 1))
                dst = take(w, ("lg", 0))
                for t in range(TPG):
                    for c in range(DC):
                        ins = pe.matmul(dst[:, t * E:(t + 1) * E], x2T[:, c, t * P:(t + 1) * P], rw_sb[:, c, :],
                                        start=(c == 0), stop=(c == DC - 1))
                ins.then_inc(work_filled, 1)

            def count_chosen(w, g):
                pe.wait_ge(chosen_ready, g + 1)
                dst = take(w, ("rt", 0))
                m = chosen[:].rearrange("p t e -> p (t e)")
                pe.matmul(dst[:, 0:TPG * E], before[:], m, start=True, stop=True)
                pe.matmul(dst[:, TPG * E:2 * TPG * E], ones[:], m, start=True, stop=True).then_inc(work_filled, 1)

            def step(g):
                w = Work(g)
                for j in range(NHALF):
                    for kind, i, lag in w.slot(j):
                        if kind == "O":
                            project(w, i)
                        elif kind == "x2T":
                            turn_x2(w, g - lag, i)
                        elif kind == "lg":
                            route_logits(w)
                        elif kind == "xT":
                            turn_x(w, g + 1, i)
                        elif kind == "q":
                            query(w, i)
                        elif kind == "pv":
                            context(w, g - lag, i)
                        elif kind == "rt":
                            count_chosen(w, g - 2)
                    if j < 2 and w.has(1):
                        turn_probs(g - 1, NHALF - 2 + j)
                    if j >= 2 and w.has(0):
                        turn_probs(g, j - 2)
                    if w.has(0):
                        scores(w, g, j)

            w = Work(-1)
            for t in range(TPG):
                turn_x(w, 0, t)
            pe.wait_ge(w_hi, DC + 2)
            pe.wait_ge(kbd_ready, 3)
            for c in range(2):
                query(w, c)
            for g in range(LOOP[0]):
                step(g)
            with pe.Fori(*LOOP) as g:
                step(g)
            for g in range(LOOP[1], ITERATIONS):
                step(g)
            pe.drain().then_inc(phase1_done, 1)
            pe.wait_ge(phase1_done, 3)

            def turn_rows(e):
                for i in range(ST):
                    pe.wait_ge(gathered[i], 16 * e + 16)
                    if i < 3:
                        first_wait(pe, h_split, e * (2 * FU))
                    else:
                        pe.wait_ge(xg_split, e * ST + i - 2)
                    for c in range(DC):
                        ins = pe.transpose(psum[:, 5 + i % 3, c * P:(c + 1) * P], xg[:, i, c * P:(c + 1) * P],
                                           ident[:])
                    ins.then_inc(xg_turned, 1)

            def up(e, u, n):
                pe.wait_ge(w1_split, e * FU + u + 1)
                for part, (cols, counts_for) in enumerate(parts_of(n)):
                    turn = len(parts_of(n)) * u + part
                    if turn < 3:
                        pe.wait_ge(xg_split, (e + 1) * ST)
                    else:
                        pe.wait_ge(h_split, e * (2 * FU) + (turn - 2) * counts_for)
                    ins = product(h_bank(n, u, part)[:, 0:cols.stop - cols.start],
                                  [(w1_h[:, u % 4, c, :], w1_l[:, u % 4, c, :], xT_h[:, c, cols], xT_l[:, c, cols])
                                   for c in range(DC)])
                    ins.then_inc(h_filled, counts_for)

            def down(e, u, n):
                pe.wait_ge(w2_split, e * FU + u + 1)
                pe.wait_ge(h_split, e * (2 * FU) + 2 * u + 2)
                wh, wl = w2_h[:, u % 4, :], w2_l[:, u % 4, :]
                for i in range(n):
                    rows = slice(i * P, (i + 1) * P)
                    hh, hl = h_h[:, u % 3, rows], h_l[:, u % 3, rows]
                    y = psum[:, i, :]
                    pe.matmul(y, hh, wh, start=(u == 0), stop=False)
                    pe.matmul(y, hh, wl, start=False, stop=False)
                    ins = pe.matmul(y, hl, wh, start=False, stop=(u == FU - 1))
                    if u == FU - 1:
                        ins.then_inc(y_filled, tile_count(n, i))
                if u < FU - 1:
                    ins.then_inc(down_done, 1)

            turn_rows(0)

            def expert(e, n):
                up(e, 0, n)
                up(e, 1, n)
                for u in range(FU):
                    if u == FU - 1:
                        turn_rows(e + 1)
                    down(e, u, n)
                    if u + 2 < FU:
                        up(e, u + 2, n)

            with pe.Fori(0, E) as e:
                by_tiles(pe, e, lambda n: expert(e, n))

        @block.vector
        def _(dve):
            steps = Steps(dve, dve_step)
            link = steps.link

            def f32(ap):
                return ap.bitcast(F32)

            dve.memset(f32(kbd_h[:]), 0.0)
            link(dve.memset(f32(kbd_l[:]), 0.0))
            dve.memset(run[:, 0, :], 0.0)
            dve.wait_ge(const_done, 9)
            dve.tensor_copy(iota_e[:], iota_i[:])
            dve.tensor_copy(tok_f[:], tok_i[:])
            link(dve.tensor_copy(trash_f[:], trash_i[:]))
            for c in range(DC):
                dve.wait_ge(w_hi, c + 1)
                dve.scalar_tensor_tensor(out=xnT_l[:, c, 0:BATCH * KEYS], in0=wbank(c % 2)[:, 0:BATCH * KEYS],
                                         scalar=bk_sb[:, c:c + 1], in1=f32(xnT_h[:, c, 0:BATCH * KEYS]),
                                         op0=ALU.add, op1=ALU.subtract).then_inc(work_drained, 1)
            for b in range(BATCH):
                dve.wait_ge(work_filled, DC + b + 1)
                dve.tensor_tensor(v_all[:, b * D:(b + 1) * D], wbank(b), bv_sb[:], ALU.add)\
                    .then_inc(work_drained, 1)
            dve.wait_ge(work_drained, PREP_USES)
            for n in range(HQ):
                rows = slice(n * DH, (n + 1) * DH)
                for src, dst in ((xnT_h, kbd_h), (xnT_l, kbd_l)):
                    ins = dve.tensor_copy(
                        dst[rows, :].rearrange("p (b c h k) -> p b c h k", b=BATCH, c=DC, h=HQ)[:, :, :, n, :],
                        f32(src[rows, :, 0:BATCH * KEYS]).rearrange("p c (b k) -> p b c k", b=BATCH))
            ins.then_inc(kbd_ready, 1)
            dve.wait_ge(w_hi, DC + 2)
            dve.tensor_tensor(wq_l[:], raw_w[0], f32(wq_h[:]), ALU.subtract).then_inc(kbd_ready, 1)
            dve.tensor_tensor(wo_l[:], raw_w[3], f32(wo_h[:]), ALU.subtract).then_inc(kbd_ready, 1)
            dve.wait_ge(tanh_done, 2)
            dve.tensor_scalar(bo_sb[:], bo_sb[:], tgx[:, 0:1], None, ALU.mult).then_inc(bo_ready, 1)
            assert steps.n == LINKS_PREP, steps.n
            steps.enter(LINKS_PREP)

            def row_stats(src, t):
                steps.mark(dve.bn_stats(stats[:, t, :], src))

            def row_means(to, a, b):
                steps.wait()
                dve.sem_inc(passed, 1)
                for t in range(a, b):
                    ins = dve.bn_aggr(to[0][:, t, :], stats[:, t, :])
                steps.mark(ins)

            def root_seed(to, a, b):
                mv, rs = to
                steps.wait()
                link(dve.tensor_scalar(ve[:, a:b], mv[:, a:b, 1], EPS, None, ALU.add))
                dve.tensor_scalar(nhv[:, a:b], ve[:, a:b], -0.5, None, ALU.mult)
                link(dve.tensor_scalar(nt[:, a:b].bitcast(I32), ve[:, a:b].bitcast(I32), 1, None,
                                       ALU.logical_shift_right))
                steps.mark(dve.tensor_scalar(rs[:, a:b].bitcast(I32), nt[:, a:b].bitcast(I32), -1.0,
                                               1597463007.0, ALU.mult, ALU.add))

            def root_round(to, a, b):
                rs = to[1]
                steps.wait()
                link(dve.tensor_tensor(nt[:, a:b], rs[:, a:b], rs[:, a:b], ALU.mult))
                link(dve.tensor_tensor(nt[:, a:b], nt[:, a:b], nhv[:, a:b], ALU.mult))
                steps.mark(dve.scalar_tensor_tensor(out=rs[:, a:b], in0=nt[:, a:b], scalar=1.5,
                                                      in1=rs[:, a:b], op0=ALU.add, op1=ALU.mult))

            def normalise(dst, src, t, to):
                mv, rs = to
                steps.wait()
                return dve.tensor_scalar(dst, src, mv[:, t, 0:1], rs[:, t:t + 1], ALU.subtract, ALU.mult)

            def x_stats(g, t):
                if t == 0:
                    dve.wait_ge(x_loaded, 16 * g + 16)
                row_stats(x_sb[:, t, :], t)

            def x_norm(t):
                normalise(xn[:, t % 2, :], x_sb[:, t, :], t, x_mv).then_inc(xn_ready, 1)

            def x_lo(w, g, t):
                dve.wait_ge(xT_hi, TPG * g + t + 1)
                ts = slice(t * P, (t + 1) * P)
                dve.tensor_tensor(xnT_l[:, :, ts], wbank(w.bank("xT", t)).rearrange("p (c n) -> p c n", c=DC),
                                  f32(xnT_h[:, :, ts]), ALU.subtract).then_inc(work_drained, 1)

            def query_lo(w, g, c):
                dve.wait_ge(q_hi, DC * g + c + 1)
                dve.scalar_tensor_tensor(out=qT_l[:, c, :], in0=wbank(w.bank("q", c)),
                                         scalar=bq_sb[:, c:c + 1], in1=f32(qT_h[:, c, :]),
                                         op0=ALU.add, op1=ALU.subtract).then_inc(work_drained, 1)

            def context_lo(w, g, c):
                dve.wait_ge(o_hi, DC * g + c + 1)
                dve.tensor_tensor(oT_l[:, c, :], wbank(w.bank("pv", c)), f32(oT_h[:, c, :]),
                                  ALU.subtract).then_inc(work_drained, 1)

            def row_max(g, j):
                b = j % 2
                dve.wait_ge(s_filled, NHALF * g + j + 1)
                steps.mark(dve.tensor_reduce(
                    nmax[:, b, :].rearrange("p (a h) -> p a h", a=2),
                    psum[:, 2 * b:2 * b + 2, :].rearrange("p a (h k) -> p a h k", h=HQ),
                    AX.X, ALU.max, negate=True))
                return steps.base + steps.n

            def scale_max(j, found):
                b = j % 2
                dve.wait_ge(dve_step, found)
                dve.tensor_scalar(nbias[:, b, :], nmax[:, b, :], SCALE, None, ALU.mult).then_inc(nbias_ready, 1)

            def reciprocals(g, j):
                b = j % 2
                dve.wait_ge(exp_done, NHALF * g + j + 1)
                dve.reciprocal(rinv[:, b, :], psums[:, b, :]).then_inc(rinv_ready, 1)

            def residual(w, g, t):
                if t == 0:
                    dve.wait_ge(xr_ready, g + 1)
                if t == 0:
                    first_wait(dve, xn2_ready, g * TPG)
                if t == 3:
                    dve.wait_ge(xn2_ready, g * TPG + 1)
                    dve.wait_ge(x2_stored[0], g * (16 * 2) + 16)
                dve.wait_ge(work_filled, w.count("O", t))
                dve.scalar_tensor_tensor(out=x2[:, t % 3, :], in0=wbank(w.bank("O", t)), scalar=tgx[:, 0:1],
                                         in1=xr[:, t, :], op0=ALU.mult, op1=ALU.add).then_inc(work_drained, 1)

            def x2_stats(w, t):
                dve.wait_ge(work_drained, w.count("O", t))
                row_stats(x2[:, t % 3, :], t)

            def x2_norm(g, t):
                if t >= 2:
                    dve.wait_ge(xn2_stored[t % 2], g * (16 * TPG // 2) + 16 * (t // 2))
                normalise(xn2[:, t % 2, :], x2[:, t % 3, :], t, pair_mv).then_inc(xn2_ready, 1)

            def take_x2T(w, t):
                dve.wait_ge(work_filled, w.count("x2T", t))
                dve.tensor_copy(x2T[:, :, t * P:(t + 1) * P],
                                wbank(w.bank("x2T", t)).rearrange("p (c n) -> p c n", c=DC))\
                    .then_inc(work_drained, 1)

            def take_logits(w):
                dve.wait_ge(work_filled, w.count("lg", 0))
                dve.tensor_tensor(logits[:], wbank(w.bank("lg", 0))[:, 0:TPG * E].rearrange(
                    "p (t e) -> p t e", t=TPG), rb_sb[:, None, :].broadcast_to([P, TPG, E]), ALU.add)\
                    .then_inc(work_drained, 1)

            def take_counts(w):
                dve.wait_ge(work_filled, w.count("rt", 0))
                dve.tensor_copy(counts[:].rearrange("p a t e -> p (a t e)"),
                                wbank(w.bank("rt", 0))[:, 0:2 * TPG * E]).then_inc(work_drained, 1)

            def choose(w, part):
                if part == 0:
                    wait_apart(dve, work_drained, w.count("lg", 0))
                    for t in range(TPG):
                        ins = dve.max(top[:, t, :], logits[:, t, :])
                    steps.mark(ins)
                elif part == 1:
                    steps.wait()
                    dve.sem_inc(passed, 1)
                    for t in range(TPG):
                        ins = dve.max_index(topi[:, t, :], top[:, t, :], logits[:, t, :])
                    steps.mark(ins)
                else:
                    steps.wait()
                    dve.tensor_tensor(vdiff[:], top[:, :, 1], top[:, :, 0], ALU.subtract).then_inc(vdiff_ready, 1)
                    link(dve.tensor_copy(topf[:], topi[:, :, 0:2].rearrange("p t k -> p k t")))
                    for k in range(2):
                        ins = dve.tensor_tensor(onehot[:, k], iota_e[:, None, :].broadcast_to([P, TPG, E]),
                                                topf[:, k, :, None].broadcast_to([P, TPG, E]), ALU.is_equal)
                    link(ins)
                    dve.tensor_tensor(chosen[:], onehot[:, 0], onehot[:, 1], ALU.add).then_inc(chosen_ready, 1)

            def place(w, g, part):
                if part == 0:
                    dve.wait_ge(work_drained, w.count("rt", 0))
                    for t in range(TPG):
                        link(dve.tensor_tensor(run[:, t + 1, :], run[:, t, :], counts[:, 1, t, :], ALU.add))
                    steps.mark(dve.tensor_tensor(pos[:], counts[:, 0], run[:, 0:TPG, :], ALU.add))
                elif part == 1:
                    steps.wait()
                    dve.tensor_copy(run[:, 0, :], run[:, TPG, :])
                    for k in range(2):
                        ins = dve.tensor_tensor(prod[:, k], onehot[:, k], pos[:], ALU.mult)
                    link(ins)
                    link(dve.tensor_reduce(pk[:], prod[:], AX.X, ALU.add))
                    dve.tensor_scalar(kept[:], pk[:], float(CAP), None, ALU.is_lt)
                    steps.mark(dve.tensor_scalar(offs[:], pk[:], float(P), None, ALU.is_ge))
                elif part == 2:
                    steps.wait()
                    for m in range(2, ST):
                        link(dve.scalar_tensor_tensor(out=offs[:], in0=pk[:], scalar=float(m * P), in1=offs[:],
                                                      op0=ALU.is_ge, op1=ALU.add))
                    link(dve.tensor_scalar(offs[:], offs[:], -float(P * ST - 1), None, ALU.mult))
                    link(dve.scalar_tensor_tensor(out=dest_f[:], in0=pk[:], scalar=float(ST), in1=offs[:],
                                                  op0=ALU.mult, op1=ALU.add))
                    steps.mark(dve.scalar_tensor_tensor(out=dest_f[:], in0=topf[:], scalar=float(CAP),
                                                          in1=dest_f[:], op0=ALU.mult, op1=ALU.add))
                elif part == 3:
                    steps.wait()
                    dve.wait_ge(gexp_done, g + 1)
                    link(dve.tensor_scalar(den[:], gexp[:], 1.0, None, ALU.add))
                    dve.tensor_tensor(dest_f[:], dest_f[:], trash_f[:], ALU.subtract)
                    link(dve.reciprocal(gk[:, 0, :], den[:]))
                    dve.tensor_tensor(dest_f[:], dest_f[:], kept[:], ALU.mult)
                    link(dve.tensor_tensor(gk[:, 1, :], gk[:, 0, :], gexp[:], ALU.mult))
                    dve.tensor_tensor(dest_f[:], dest_f[:], trash_f[:], ALU.add)
                    link(dve.tensor_tensor(gk[:], gk[:], kept[:], ALU.mult))
                    steps.mark(dve.tensor_tensor(den[:], gk[:, 0, :], gk[:, 1, :], ALU.add))
                else:
                    steps.wait()
                    link(dve.tensor_scalar(den[:], den[:], 1e-9, None, ALU.add))
                    link(dve.reciprocal(den[:], den[:]))
                    for k in range(2):
                        ins = dve.tensor_tensor(gk[:, k, :], gk[:, k, :], den[:], ALU.mult)
                    link(ins)
                    dve.wait_ge(entry_free, g + 1)
                    dve.tensor_copy(dest[:], dest_f[:])
                    for k in range(2):
                        dve.tensor_copy(entry[:, k, :, 0], tok_f[:])
                    link(dve.tensor_scalar(entry[:, :, :, 1].bitcast(F32), gk[:], tgf[:, 0:1], None, ALU.mult))
                    dve.tensor_scalar(tok_f[:], tok_f[:], float(GT), None, ALU.add)
                    dve.tensor_scalar(trash_f[:], trash_f[:], float(GT), None, ALU.add).then_inc(entry_ready, 1)

            def piece(w, g, name):
                what, *rest = name.split()
                i = int(rest[-1]) if rest and rest[-1].isdigit() else None
                if what == "v":
                    if w.has(0):
                        dve.tensor_scalar(v_cur[:], v_all[:, bass.ds((g // GPB) * D, D)], 1.0, None, ALU.mult)\
                            .then_inc(v_ready, 1)
                elif what == "c":
                    if w.has(2):
                        choose(w, i)
                elif what == "t":
                    if w.has(2):
                        place(w, g - 2, i)
                elif w.has({"x": -1, "p": 1, "r": 1}[what]):
                    to, a, b = {"x": (x_mv, 0, TPG), "p": (pair_mv, 0, 2), "r": (pair_mv, 2, 4)}[what]
                    if rest[0] == "stats":
                        x_stats(g + 1, i) if what == "x" else x2_stats(w, i)
                    elif rest[0] == "mean":
                        row_means(to, a, b)
                    elif rest[0] == "seed":
                        root_seed(to, a, b)
                    elif rest[0] == "root":
                        root_round(to, a, b)
                    else:
                        x_norm(i) if what == "x" else x2_norm(g - 1, i)

            def drain(w, g, kind, i, lag):
                if kind == "O":
                    residual(w, g - 1, i)
                elif kind == "x2T":
                    take_x2T(w, i)
                elif kind == "lg":
                    take_logits(w)
                elif kind == "xT":
                    x_lo(w, g + 1, i)
                elif kind == "q":
                    query_lo(w, g - lag, i)
                elif kind == "pv":
                    context_lo(w, g - lag, i)
                elif kind == "rt":
                    take_counts(w)

            def step(g, links):
                steps.enter(links)
                w = Work(g)
                for j in range(NHALF):
                    *after_use, before_scaling, at_end = SIDE[j]
                    for use, pieces in zip(SLOTS[j], after_use):
                        if w.has(use[2]):
                            drain(w, g, *use)
                        for name in pieces:
                            piece(w, g, name)
                    if j >= 1 and w.has(0):
                        reciprocals(g, j - 1)
                    if j == 0 and w.has(1):
                        reciprocals(g - 1, NHALF - 1)
                    if w.has(0):
                        found = row_max(g, j)
                    for name in before_scaling:
                        piece(w, g, name)
                    if w.has(0):
                        scale_max(j, found)
                    for name in at_end:
                        piece(w, g, name)
                assert steps.n == links_of(g), (steps.n, links_of(g))

            w = Work(-1)
            for t in range(TPG):
                x_stats(0, t)
            row_means(x_mv, 0, TPG)
            root_seed(x_mv, 0, TPG)
            for _ in range(3):
                root_round(x_mv, 0, TPG)
            for t in range(TPG):
                if t >= 2:
                    x_lo(w, 0, t - 2)
                x_norm(t)
            x_lo(w, 0, 2)
            x_lo(w, 0, 3)
            for c in range(2):
                query_lo(w, 0, c)
            base = LINKS_PREP + links_of(-1)
            for g in range(LOOP[0]):
                step(g, base)
                base += links_of(g)
            with dve.Fori(*LOOP) as g:
                step(g, (g - LOOP[0]) * links_of(g) + base)
            base += links_of(LOOP[0]) * (LOOP[1] - LOOP[0])
            for g in range(LOOP[1], ITERATIONS):
                step(g, base)
                base += links_of(g)
            steps.enter(base)
            steps.wait()
            link(dve.tensor_scalar(pos[:, 0, :], run[:, 0, :], float(LEAST * P), None, ALU.is_gt))
            for m in range(LEAST + 1, ST):
                link(dve.scalar_tensor_tensor(out=pos[:, 0, :], in0=run[:, 0, :], scalar=float(m * P),
                                              in1=pos[:, 0, :], op0=ALU.is_gt, op1=ALU.add))
            dve.tensor_scalar(n_tiles[:], pos[:, 0, :], float(LEAST), None, ALU.add)
            dve.drain().then_inc(phase1_done, 1)
            dve.wait_ge(phase1_done, 3)

            def weights_lo(u, e):
                r, n, k = (u // UPL) % NRAW, u % UPL, e * FU + u + 1
                dve.wait_ge(w1_hi, k)
                dve.tensor_tensor(w1_l[:, u % 4], raw1[:, r, n * D:(n + 1) * D].rearrange("p (c n) -> p c n", c=DC),
                                  f32(w1_h[:, u % 4]), ALU.subtract).then_inc(w1_split, 1)
                dve.wait_ge(w2_hi, k)
                dve.tensor_tensor(w2_l[:, u % 4], raw2[:, r, n * D:(n + 1) * D], f32(w2_h[:, u % 4]),
                                  ALU.subtract).then_inc(w2_split, 1)

            def rows_lo(e, i):
                dve.wait_ge(xg_hi, e * ST + i + 1)
                cols = slice(i * P, (i + 1) * P)
                dve.tensor_tensor(xT_l[:, :, cols], psum[:, 5 + i % 3, :].rearrange("p (c n) -> p c n", c=DC),
                                  f32(xT_h[:, :, cols]), ALU.subtract).then_inc(xg_split, 1)

            weights_lo(0, 0)
            weights_lo(1, 0)
            for i in range(ST):
                rows_lo(0, i)

            def expert(e, n):
                for u in range(FU):
                    weights_lo(u + 2, e)
                    for part, (cols, counts_for) in enumerate(parts_of(n)):
                        dve.wait_ge(h_gelu, e * (2 * FU) + 2 * u + part + counts_for)
                        dve.tensor_tensor(h_l[:, u % 3, cols], h_f[:, u % 3, cols], f32(h_h[:, u % 3, cols]),
                                          ALU.subtract).then_inc(h_split, counts_for)
                for i in range(ST):
                    rows_lo(e + 1, i)
                dve.wait_ge(b2_loaded, 16 * e + 16)
                for i in range(n):
                    dve.wait_ge(y_filled, e * ST + i + 1)
                    dve.tensor_tensor(y_sb[:, i, :], psum[:, i, :], b2_sb[:], ALU.add)\
                        .then_inc(y_biased, tile_count(n, i))

            with dve.Fori(0, E) as e:
                dve.tensor_scalar(b1_cur[:], b1_sb[:, bass.ds(e * FU, FU)], 1.0, None, ALU.mult)\
                    .then_inc(b1_taken, 1)
                by_tiles(dve, e, lambda n: expert(e, n))


def _cols(v):
    import numpy as np
    return np.ascontiguousarray(v.reshape(-1, P).T)


def kernel(x, ctx_1024, g_xattn, g_ffn, L0_xattn_w_q, L0_xattn_b_q, L0_xattn_w_k, L0_xattn_b_k, L0_xattn_w_v,
           L0_xattn_b_v, L0_xattn_w_o, L0_xattn_b_o, L0_ffn_router_w, L0_ffn_router_b, L0_ffn_w1, L0_ffn_b1,
           L0_ffn_w2, L0_ffn_b2):
    import numpy as np
    import concourse.bacc as bacc
    from concourse.bass_utils import run_bass_kernel_spmd

    def t(a):
        return np.ascontiguousarray(np.asarray(a).T)

    w1 = np.asarray(L0_ffn_w1).reshape(E, DC, P, PAIRS, UPL, P).transpose(0, 3, 2, 4, 1, 5)
    w2 = np.asarray(L0_ffn_w2).reshape(E, PAIRS, UPL, P, D).transpose(0, 1, 3, 2, 4)
    ins = [
        ("x", np.asarray(x).reshape(TOK, D)),
        ("ctxT", t(np.asarray(ctx_1024).reshape(BATCH * KEYS, D))),
        ("gx", np.asarray(g_xattn).reshape(1, 1)),
        ("gf", np.asarray(g_ffn).reshape(1, 1)),
        ("wqT", t(L0_xattn_w_q)), ("bq", _cols(np.asarray(L0_xattn_b_q))),
        ("wkT", t(L0_xattn_w_k)), ("bk", _cols(np.asarray(L0_xattn_b_k))),
        ("wvT", t(L0_xattn_w_v)), ("bv", np.asarray(L0_xattn_b_v).reshape(1, D)),
        ("woT", t(L0_xattn_w_o)), ("bo", np.asarray(L0_xattn_b_o).reshape(1, D)),
        ("rwT", t(L0_ffn_router_w)), ("rb", np.asarray(L0_ffn_router_b).reshape(1, E)),
        ("w1", np.ascontiguousarray(w1).reshape(E * PAIRS, P, UPL * D)),
        ("b1", _cols(np.asarray(L0_ffn_b1))),
        ("w2", np.ascontiguousarray(w2).reshape(E * PAIRS, P, UPL * D)),
        ("b2", np.asarray(L0_ffn_b2)),
    ]
    nc = bacc.Bacc("TRN2", target_bir_lowering=False, num_devices=1)
    arrays, args = {}, []
    for name, a in ins:
        a = np.ascontiguousarray(a)
        arrays["in_" + name] = a
        args.append(nc.dram_tensor("in_" + name, a.shape, mybir.dt.from_np(a.dtype), kind="ExternalInput").ap())
    args.append(nc.dram_tensor("out_rows", [TOK + CAP, D], F32, kind="ExternalOutput").ap())
    build(nc, *args)
    r = run_bass_kernel_spmd(nc, [arrays], core_ids=[0])
    return r.results[0]["out_rows"][:TOK].reshape(BATCH, SEQ, D)
```

```python
import concourse.bass as bass
from concourse import mybir
from contextlib import ExitStack

F32 = mybir.dt.float32
F32R = mybir.dt.float32r
I32 = mybir.dt.int32
U32 = mybir.dt.uint32
ALU = mybir.AluOpType
ACT = mybir.ActivationFunctionType
AX = mybir.AxisListType

P = 128
D = 512
DC = D // P
H = 16
DH = D // H
HQ = P // DH
KEYS = 128
BATCH = 2
SEQ = 2048
TOK = BATCH * SEQ
GT = 512
TPG = GT // P
G = TOK // GT
GPB = SEQ // GT
NHALF = 2 * TPG
HH = H // 2
SCALE = DH ** -0.5
EPS = 1e-5

E = 16
F = 2048
FU = F // P
CAP = -(-5 * TOK * 2 // (4 * E))
ST = CAP // P
UPL = 2
PAIRS = FU // UPL
NRAW = 4
TABLE = (E + 1) * CAP
assert CAP % P == 0
STEP = 64
STEPS = CAP // STEP
LEAST = 256 // STEP

SLOTS = [
    [("q", 2, 0), ("pv", 0, 1)],
    [("q", 3, 0), ("pv", 1, 1), ("x2T", 2, 2), ("x2T", 3, 2)],
    [("pv", 2, 1), ("pv", 3, 1), ("xT", 0, -1), ("lg", 0, 2)],
    [("O", 0, 1), ("xT", 1, -1)],
    [("O", 1, 1), ("rt", 0, 2), ("xT", 2, -1)],
    [("O", 2, 1), ("xT", 3, -1)],
    [("O", 3, 1), ("x2T", 0, 1)],
    [("q", 0, -1), ("x2T", 1, 1), ("q", 1, -1)],
]
SIDE = [
    [["x stats 0"], [], ["x stats 1"], ["x stats 2", "x stats 3"]],
    [["x mean"], [], [], ["x seed"], ["x root 0"], ["x root 1", "x root 2", "x norm 0"]],
    [[], [], [], [], ["x norm 1"], ["c 0"]],
    [["p stats 0"], [], [], ["x norm 2", "c 1", "c 2", "v"]],
    [["p stats 1"], [], [], [], ["x norm 3", "p mean", "p seed", "t 0"]],
    [["r stats 2", "p root 0"], [], [], ["p root 1", "p root 2", "p norm 0", "p norm 1"]],
    [[], [], [], ["r stats 3", "r mean", "r seed", "t 1"]],
    [["r root 0", "t 2"], [], ["r root 1", "r root 2"], ["t 3"], ["r norm 2", "r norm 3", "t 4"]],
]
SIDE_LAG = {"x": -1, "p": 1, "r": 1, "c": 2, "t": 2, "v": 0}
SIDE_LINKS = {"stats": 1, "mean": 1, "seed": 3, "root": 3, "norm": 0, "v": 0,
              "c": (1, 1, 2), "t": (5, 3, 6, 5, 4)}
PREP_USES = 6
ITERATIONS = G + 2
LOOP = (2, G - 1)


def uses_of(g):
    def there(u):
        return not isinstance(g, int) or 0 <= g - u[2] < G
    return [u for slot in SLOTS for u in slot if there(u)]


ALL_USES = sum(len(slot) for slot in SLOTS)
LOOP_BASE = PREP_USES + sum(len(uses_of(g)) for g in range(-1, LOOP[0]))


class Work:

    def __init__(self, g):
        self.order = [u[:2] for u in uses_of(g)]
        if isinstance(g, int):
            self.base = PREP_USES + sum(len(uses_of(i)) for i in range(-1, g))
            self.parity = self.base % 2
        else:
            self.base = (g - LOOP[0]) * ALL_USES + LOOP_BASE
            self.parity = LOOP_BASE % 2
        self.g = g

    def has(self, lag):
        return not isinstance(self.g, int) or 0 <= self.g - lag < G

    def bank(self, *use):
        return (self.parity + self.order.index(use)) % 2

    def count(self, *use):
        return self.base + self.order.index(use) + 1

    def count_before(self, *use):
        if isinstance(self.g, int):
            return Work(self.g - 1).count(*use)
        return self.count(*use) - ALL_USES


class Steps:

    def __init__(self, eng, sem):
        self.eng, self.sem, self.base, self.n = eng, sem, 0, 0

    def mark(self, ins):
        self.n += 1
        ins.then_inc(self.sem, 1)

    def wait(self):
        self.eng.wait_ge(self.sem, self.base + self.n)

    def link(self, ins):
        self.mark(ins)
        self.wait()

    def enter(self, base):
        self.base, self.n = base, 0


LINKS_PREP = 2


def links_of(g):
    def has(lag):
        return not isinstance(g, int) or 0 <= g - lag < G
    n = has(0) * NHALF
    for name in [name for slot in SIDE for pieces in slot for name in pieces]:
        what, *rest = name.split()
        if has(SIDE_LAG[what]):
            links = SIDE_LINKS[what if what in SIDE_LINKS else rest[0]]
            n += links[int(rest[0])] if isinstance(links, tuple) else links
    return n


def build(nc, x, ctxT, gx, gf, wqT, bq, wkT, bk, wvT, bv, woT, bo, rwT, rb, w1, b1, w2, b2, out):
    xn_dram = nc.dram_tensor("xn_rows", [TOK + CAP, D], F32, kind="Internal").ap()
    table = nc.dram_tensor("slot_table", [TABLE + 2 * TOK, 2], I32, kind="Internal").ap()

    ctx = ExitStack()
    with ctx:
        def sem(name):
            return ctx.enter_context(nc.semaphore(name))

        psum = ctx.enter_context(nc.psum_tensor("banks", [P, 8, 512], F32))

        def wbank(b):
            return psum[:, 4 + b, :]

        ident = ctx.enter_context(nc.sbuf_tensor("ident", [P, P], F32))
        tgx = ctx.enter_context(nc.sbuf_tensor("tanh_gx", [P, 1], F32))
        tgf = ctx.enter_context(nc.sbuf_tensor("tanh_gf", [P, 1], F32))
        n_steps = ctx.enter_context(nc.sbuf_tensor("n_steps", [P, E], I32))
        b1_sb = ctx.enter_context(nc.sbuf_tensor("b1_cols", [P, (E + 1) * FU], F32))

        with ExitStack() as one:
            def sb(name, shape, dt=F32):
                return one.enter_context(nc.sbuf_tensor(name, shape, dt))

            kbd_h = sb("kbd_h", [P, BATCH * DC * HQ * KEYS], F32R)
            kbd_l = sb("kbd_l", [P, BATCH * DC * HQ * KEYS], F32R)
            before = sb("strict_upper", [P, P])
            ones = sb("ones", [P, P])
            iota_e = sb("iota_e", [P, E])
            iota_i = sb("iota_i", [P, E], I32)
            tok_i = sb("tok_i", [P, TPG], I32)
            trash_i = sb("trash_i", [P, 2, TPG], I32)
            tok_f = sb("tok_f", [P, TPG])
            trash_f = sb("trash_f", [P, 2, TPG])
            gates_in = sb("gates_in", [P, 2])
            bq_sb = sb("bq_sb", [P, DC])
            bk_sb = sb("bk_sb", [P, DC])
            bv_sb = sb("bv_sb", [P, D])
            bo_sb = sb("bo_sb", [P, D])
            rb_sb = sb("rb_sb", [P, E])
            rw_sb = sb("rw_sb", [P, DC, E])
            wq_h = sb("wq_h", [P, DC, D], F32R)
            wq_l = sb("wq_l", [P, DC, D], F32R)
            wo_h = sb("wo_h", [P, DC, D], F32R)
            wo_l = sb("wo_l", [P, DC, D], F32R)
            v_all = sb("v_all", [P, BATCH * D])
            v_cur = sb("v_cur", [P, D])
            x_sb = sb("x_sb", [P, TPG, D])
            xr = sb("xr", [P, TPG, D])
            xn = sb("xn", [P, 2, D])
            xnT_h = sb("xnT_h", [P, DC, GT], F32R)
            xnT_l = sb("xnT_l", [P, DC, GT], F32R)
            qT_h = sb("qT_h", [P, DC, GT], F32R)
            qT_l = sb("qT_l", [P, DC, GT], F32R)
            prob = sb("prob", [P, 2, HH, KEYS])
            probT = sb("probT", [P, H, GT])
            oT_h = sb("oT_h", [P, DC, GT], F32R)
            oT_l = sb("oT_l", [P, DC, GT], F32R)
            x2 = sb("x2", [P, 3, D])
            xn2 = sb("xn2", [P, 2, D])
            x2T = sb("x2T", [P, DC, GT])
            stats = sb("stats", [P, TPG, 6])
            x_mv = sb("x_mean_var", [P, TPG, 2]), sb("x_rstd", [P, TPG])
            pair_mv = sb("x2_mean_var", [P, TPG, 2]), sb("x2_rstd", [P, TPG])
            ve = sb("ve", [P, TPG])
            nhv = sb("neg_half_var", [P, TPG])
            nt = sb("newton", [P, TPG])
            nmax = sb("nmax", [P, 2, HH])
            nbias = sb("nbias", [P, 2, HH])
            psums = sb("prob_sums", [P, 2, HH])
            rinv = sb("rinv", [P, 2, HH])
            logits = sb("logits", [P, TPG, E])
            top = sb("top", [P, TPG, 8])
            topi = sb("topi", [P, TPG, 8], U32)
            topf = sb("topf", [P, 2, TPG])
            onehot = sb("onehot", [P, 2, TPG, E])
            chosen = sb("chosen", [P, TPG, E])
            run = sb("running_base", [P, TPG + 1, E])
            counts = sb("counts", [P, 2, TPG, E])
            pos = sb("pos", [P, TPG, E])
            prod = sb("prod", [P, 2, TPG, E])
            pk = sb("pk", [P, 2, TPG])
            kept = sb("kept", [P, 2, TPG])
            offs = sb("offs", [P, 2, TPG])
            dest_f = sb("dest_f", [P, 2, TPG])
            dest = sb("dest", [P, 2, TPG], I32)
            entry = sb("entry", [P, 2, TPG, 2], I32)
            vdiff = sb("vdiff", [P, TPG])
            gexp = sb("gexp", [P, TPG])
            gk = sb("gk", [P, 2, TPG])
            den = sb("den", [P, TPG])

        raw_w = [probT[:, 4 * i:4 * i + 4, :] for i in range(4)]
        ctx_sb = x2T[:, :, 0:BATCH * KEYS]
        fill = prob[:, :, :, :].rearrange("p a h k -> p (a h k)").bitcast(I32)

        with ExitStack() as two:
            def sb(name, shape, dt=F32):
                return two.enter_context(nc.sbuf_tensor(name, shape, dt))

            raw1 = sb("raw_w1", [P, NRAW, UPL * D])
            raw2 = sb("raw_w2", [P, NRAW, UPL * D])
            w1_h = sb("w1_h", [P, 4, DC, P], F32R)
            w1_l = sb("w1_l", [P, 4, DC, P], F32R)
            w2_h = sb("w2_h", [P, 4, D], F32R)
            w2_l = sb("w2_l", [P, 4, D], F32R)
            xg = sb("xg", [P, ST, D])
            xT_h = sb("xT_h", [P, DC, CAP], F32R)
            xT_l = sb("xT_l", [P, DC, CAP], F32R)
            h_f = sb("h_f", [P, 3, CAP])
            h_h = sb("h_h", [P, 3, CAP], F32R)
            h_l = sb("h_l", [P, 3, CAP], F32R)
            y_sb = sb("y_sb", [P, ST, D])
            y_w = sb("y_w", [P, ST, D])
            b2_sb = sb("b2_sb", [P, D])
            b1_cur = sb("b1_cur", [P, FU])
            tab_next = sb("tab_next", [P, ST, 2], I32)
            tab_cur = sb("tab_cur", [P, ST, 2], I32)

        const_done = sem("const_done")
        w_loaded = {name: sem(f"{name}_loaded") for name in ("ctx", "wk", "wv", "wq", "wo")}
        bk_loaded = sem("bk_loaded")
        small_loaded = sem("small_loaded")
        w_hi = sem("w_hi")
        kbd_ready = sem("kbd_ready")
        wq_split = sem("wq_split")
        wo_split = sem("wo_split")
        bo_ready = sem("bo_ready")
        tanh_done = sem("tanh_done")
        fill_ready = sem("fill_ready")
        init_stored = sem("init_stored")
        x_loaded = sem("x_loaded")
        xr_loaded = sem("xr_loaded")
        xr_ready = sem("xr_ready")
        dve_step = sem("dve_step")
        xn_ready = sem("xn_ready")
        work_filled = sem("work_filled")
        work_drained = sem("work_drained")
        xT_hi = sem("xT_hi")
        q_hi = sem("q_hi")
        o_hi = sem("o_hi")
        s_filled = sem("s_filled")
        nbias_ready = sem("nbias_ready")
        exp_done = sem("exp_done")
        prob_ready = sem("prob_ready")
        pT_filled = sem("pT_filled")
        pT_taken = sem("pT_taken")
        rinv_ready = sem("rinv_ready")
        v_ready = sem("v_ready")
        xn2_ready = sem("xn2_ready")
        x2_stored = [sem(f"x2_stored{i}") for i in range(2)]
        xn2_stored = [sem(f"xn2_stored{i}") for i in range(2)]
        chosen_ready = sem("chosen_ready")
        vdiff_ready = sem("vdiff_ready")
        gexp_done = sem("gexp_done")
        entry_ready = sem("entry_ready")
        scattered = sem("scattered")
        entry_free = sem("entry_free")
        phase1_done = sem("phase1_done")

        raw_loaded = [sem(f"raw_loaded{i}") for i in range(NRAW)]
        w1_hi = sem("w1_hi")
        w1_split = sem("w1_split")
        w2_hi = sem("w2_hi")
        w2_split = sem("w2_split")
        tab_loaded = sem("tab_loaded")
        tab_taken = sem("tab_taken")
        gathered = [sem(f"gathered{i}") for i in range(ST)]
        xg_turned = sem("xg_turned")
        xg_hi = sem("xg_hi")
        xg_split = sem("xg_split")
        h_filled = sem("h_filled")
        h_gelu = sem("h_gelu")
        h_split = sem("h_split")
        down_done = sem("down_done")
        y_filled = sem("y_filled")
        y_biased = sem("y_biased")
        y_free = sem("y_free")
        y_weighted = sem("y_weighted")
        b2_loaded = sem("b2_loaded")
        added = sem("added")
        passed = sem("passed")
        b1_taken = sem("b1_taken")

        def wait_apart(eng, s, value):
            eng.wait_ge(s, value)
            eng.sem_inc(passed, 1)

        def first_wait(eng, s, value):
            if not isinstance(value, int) or value > 0:
                eng.wait_ge(s, value)

        def parts_of(n):
            cols = n * STEP
            if cols <= 512:
                return [(slice(0, cols), 2)]
            return [(slice(0, cols // 2), 1), (slice(cols // 2, cols), 1)]

        def h_bank(n, u, part):
            return psum[:, 5 + (len(parts_of(n)) * u + part) % 3, :]

        def rows_bank(n, i):
            return psum[:, 5 + ((len(parts_of(n)) * FU if n else 0) + i) % 3, :]

        def early_rows(n):
            return 3 - len(parts_of(n))

        def tiles_of(n):
            tiles = -(-n * STEP // P)
            return [(i, min(P, n * STEP - i * P), 1 if i < tiles - 1 else 1 + ST - tiles) for i in range(tiles)]

        def by_steps(eng, e, body):
            found = eng.value_load(n_steps[0:1, bass.ds(e, 1)], min_val=LEAST, max_val=STEPS)
            for n in range(LEAST, STEPS + 1):
                with eng.If(found == n):
                    body(n)

        def rows_of(t, g):
            return t[bass.ds(g * GT, GT), :].rearrange("(t p) n -> p t n", p=P)

        block = ctx.enter_context(nc.Block())

        @block.sync
        def _(sp):
            def load_matrix(name, dst, src):
                sp.dma_start(dst, src.rearrange("(c p) n -> p c n", p=P)).then_inc(w_loaded[name], 16)

            load_matrix("ctx", ctx_sb, ctxT)
            load_matrix("wk", raw_w[1], wkT)
            sp.dma_start(bk_sb[:], bk).then_inc(bk_loaded, 16)
            load_matrix("wv", raw_w[2], wvT)
            sp.dma_start(x_sb[:], rows_of(x, 0)).then_inc(x_loaded, 16)
            load_matrix("wq", raw_w[0], wqT)
            sp.dma_start(bq_sb[:], bq).then_inc(small_loaded, 16)
            for dst, src in ((bv_sb[:], bv), (bo_sb[:], bo), (rb_sb[:], rb),
                             (gates_in[:, 0:1], gx), (gates_in[:, 1:2], gf)):
                sp.dma_start(dst, src.broadcast_to(list(dst.shape))).then_inc(small_loaded, 16)
            sp.dma_start(rw_sb[:], rwT.rearrange("(c p) n -> p c n", p=P)).then_inc(small_loaded, 16)
            sp.dma_start(b1_sb[:, 0:E * FU], b1).then_inc(small_loaded, 16)
            sp.dma_start(b1_sb[:, E * FU:], b1[:, 0:FU]).then_inc(small_loaded, 16)
            load_matrix("wo", raw_w[3], woT)
            sp.dma_start(xr[:], rows_of(x, 0)).then_inc(xr_loaded, 16)
            sp.wait_ge(fill_ready, 2)
            sp.dma_start(table[0:TABLE, :].rearrange("(e s) w -> e (s w)", s=CAP),
                         fill[0:E + 1, 0:2 * CAP]).then_inc(init_stored, 16)
            for i in range(ST):
                rows = slice(TOK + i * P, TOK + (i + 1) * P)
                sp.dma_start(xn_dram[rows, :], x2[:, 0, :]).then_inc(init_stored, 16)
                sp.dma_start(out[rows, :], x2[:, 0, :]).then_inc(init_stored, 16)

            def load_x(g):
                sp.wait_ge(xn_ready, TPG * g)
                sp.dma_start(x_sb[:], rows_of(x, g)).then_inc(x_loaded, 16)

            def store_x2(w, g, t):
                sp.wait_ge(work_drained, w.count("O", t))
                sp.dma_start(out[bass.ds(g * GT + t * P, P), :], x2[:, t % 3, :])\
                    .then_inc(x2_stored[min(t % 3, 1)], 16)

            def store_xn2(g, t):
                sp.wait_ge(xn2_ready, g * TPG + t + 1)
                sp.dma_start(xn_dram[bass.ds(g * GT + t * P, P), :], xn2[:, t % 2, :])\
                    .then_inc(xn2_stored[t % 2], 16)

            def loads_and_stores(g):
                w = Work(g)
                if w.has(1):
                    for t in range(3):
                        store_x2(w, g - 1, t)
                    for t in range(2):
                        store_xn2(g - 1, t)
                if w.has(-2):
                    load_x(g + 2)
                if w.has(1):
                    store_x2(w, g - 1, 3)
                    if w.has(0):
                        sp.dma_start(xr[:], rows_of(x, g)).then_inc(xr_loaded, 16)
                    for t in range(2, TPG):
                        store_xn2(g - 1, t)
            load_x(1)
            for g in range(LOOP[0]):
                loads_and_stores(g)
            with sp.Fori(LOOP[0], G - 2) as g:
                loads_and_stores(g)
            for g in range(G - 2, G + 1):
                loads_and_stores(g)

            sp.wait_ge(s_filled, NHALF * G)

            def load_weights(e, pair, turn):
                r = pair % NRAW
                if turn is not None:
                    sp.wait_ge(w1_split, turn)
                    sp.wait_ge(w2_split, turn)
                src = bass.ds(e * PAIRS + pair, 1)
                sp.dma_start(raw1[:, r, :], w1[src].rearrange("a p n -> p (a n)")).then_inc(raw_loaded[r], 16)
                sp.dma_start(raw2[:, r, :], w2[src].rearrange("a p n -> p (a n)")).then_inc(raw_loaded[r], 16)

            for pair in range(NRAW):
                load_weights(0, pair, None)
            with sp.Fori(0, E - 1) as e:
                for pair in range(PAIRS):
                    ahead = pair + NRAW
                    load_weights(e + ahead // PAIRS, ahead % PAIRS, e * FU + UPL * (pair + 1))
                    if pair == NRAW:
                        sp.dma_start(b2_sb[:], b2[bass.ds(e, 1), :].broadcast_to([P, D])).then_inc(b2_loaded, 16)
            for pair in range(PAIRS - NRAW):
                load_weights(E - 1, pair + NRAW, (E - 1) * FU + UPL * (pair + 1))
            load_weights(E - 1, 0, (E - 1) * FU + UPL * (PAIRS - NRAW + 1))
            sp.dma_start(b2_sb[:], b2[E - 1:E, :].broadcast_to([P, D])).then_inc(b2_loaded, 16)

        @block.gpsimd
        def _(pool):
            pool.memset(ident[:], 0.0).then_inc(const_done, 1)
            pool.memset(before[:], 0.0).then_inc(const_done, 1)
            pool.memset(ones[:], 1.0).then_inc(const_done, 1)
            pool.wait_ge(const_done, 3)
            pool.affine_select(out=ident[:], in_=ident[:], compare_op=ALU.not_equal, fill=1.0, base=0,
                               pattern=[[-1, P]], channel_multiplier=1).then_inc(const_done, 1)
            pool.affine_select(out=before[:], in_=before[:], compare_op=ALU.is_ge, fill=1.0, base=0,
                               pattern=[[-1, P]], channel_multiplier=1).then_inc(const_done, 1)
            pool.iota(iota_i[:], pattern=[[1, E]], base=0, channel_multiplier=0).then_inc(const_done, 1)
            pool.iota(tok_i[:], pattern=[[P, TPG]], base=0, channel_multiplier=1).then_inc(const_done, 1)
            pool.iota(trash_i[:], pattern=[[TOK, 2], [P, TPG]], base=TABLE, channel_multiplier=1)\
                .then_inc(const_done, 1)
            pool.memset(x2[:, 0, :], 0.0).then_inc(fill_ready, 1)
            pool.memset(fill[0:E + 1, 0:2 * CAP], 0).then_inc(const_done, 1)
            pool.wait_ge(const_done, 9)
            pool.iota(fill[0:E + 1, 0:2 * CAP:2], pattern=[[1, CAP]], base=TOK, channel_multiplier=0)\
                .then_inc(fill_ready, 1)

            def add_bo(g):
                pool.wait_ge(xr_loaded, 16 * g + 16)
                pool.tensor_tensor(xr[:], xr[:], bo_sb[:, None, :].broadcast_to([P, TPG, D]), ALU.add)\
                    .then_inc(xr_ready, 1)

            def scatter(g, t):
                wait_apart(pool, entry_ready, g + 1)
                for k in range(2):
                    pool.indirect_dma_start(
                        out=table[:, :], out_offset=bass.IndirectOffsetOnAxis(ap=dest[:, k, t:t + 1], axis=0),
                        in_=entry[:, k, t, :], in_offset=None).then_inc(scattered, 16)

            def softmax_norm(g, j):
                pool.wait_ge(rinv_ready, NHALF * g + j + 1)
                pool.tensor_tensor(prob[:, j % 2], prob[:, j % 2],
                                   rinv[:, j % 2, :, None].broadcast_to([P, HH, KEYS]), ALU.mult)\
                    .then_inc(prob_ready, 1)

            def step(g):
                w = Work(g)
                for j in range(NHALF):
                    if j >= 1 and w.has(0):
                        softmax_norm(g, j - 1)
                    if j == 0 and w.has(1):
                        softmax_norm(g - 1, NHALF - 1)
                        add_bo(g - 1)
                    if 1 <= j < 1 + TPG and w.has(3):
                        scatter(g - 3, j - 1)
                    if j == 6 and w.has(3):
                        pool.wait_ge(scattered, (g - 2) * (16 * 2 * TPG))
                        pool.sem_inc(entry_free, 1)

            pool.wait_ge(bo_ready, 1)
            pool.wait_ge(init_stored, 16 * (1 + 2 * ST))
            pool.sem_inc(entry_free, 1)
            for g in range(LOOP[0] + 1):
                step(g)
            with pool.Fori(LOOP[0] + 1, LOOP[1]) as g:
                step(g)
            for g in range(LOOP[1], ITERATIONS + 1):
                step(g)
            pool.wait_ge(phase1_done, 3)
            for i in range(2):
                pool.wait_ge(x2_stored[i], 16 * TPG // 2 * G)
                pool.wait_ge(xn2_stored[i], 16 * TPG // 2 * G)

            def load_table(e):
                pool.dma_start(tab_next[:], table[bass.ds(e * CAP, CAP), :].rearrange("(p i) w -> p i w", i=ST))\
                    .then_inc(tab_loaded, 16)

            def gather(e):
                wait_apart(pool, tab_loaded, 16 * e + 16)
                for i in range(ST):
                    pool.indirect_dma_start(
                        out=xg[:, i, :], out_offset=None, in_=xn_dram[:, :],
                        in_offset=bass.IndirectOffsetOnAxis(ap=tab_next[:, i, 0:1], axis=0))\
                        .then_inc(gathered[i], 16)

            additions = pool.alloc_register("additions")
            pool.reg_mov(additions, 0)
            pool.sem_inc(y_free, 1)
            load_table(0)
            gather(0)
            with pool.Fori(0, E) as e:
                pool.tensor_copy(tab_cur[:], tab_next[:]).then_inc(tab_taken, 1)
                pool.wait_ge(tab_taken, e + 1)
                for i in range(ST):
                    pool.wait_ge(gathered[i], 16 * e + 16)
                load_table(e + 1)
                pool.wait_ge(xg_turned, ST * (e + 1))
                gather(e + 1)

                def add_rows(n):
                    for i, rows, counts_for in tiles_of(n):
                        wait_apart(pool, y_biased, e * ST + i + 1)
                        pool.tensor_scalar(y_w[0:rows, i, :], y_sb[0:rows, i, :],
                                           tab_cur[0:rows, i, 1:2].bitcast(F32), None,
                                           ALU.mult).then_inc(y_weighted, counts_for)
                        wait_apart(pool, y_weighted, e * ST + i + 1)
                        pool.indirect_dma_start(
                            out=out[:, :],
                            out_offset=bass.IndirectOffsetOnAxis(ap=tab_cur[0:rows, i, 0:1], axis=0),
                            in_=y_w[0:rows, i, :], in_offset=None, compute_op=ALU.add).then_inc(added, 16)
                        pool.reg_add(additions, additions, 16)
                    pool.wait_ge(added, additions)

                by_steps(pool, e, add_rows)
                pool.sem_inc(y_free, 1)
            for i in range(ST):
                pool.wait_ge(gathered[i], 16 * (E + 1))

        @block.scalar
        def _(act):
            act.wait_ge(bk_loaded, 16)
            for c in range(DC):
                act.wait_ge(work_filled, c + 1)
                act.activation(xnT_h[:, c, 0:BATCH * KEYS], wbank(c % 2)[:, 0:BATCH * KEYS], ACT.Identity,
                               bias=bk_sb[:, c:c + 1]).then_inc(w_hi, 1)
            act.wait_ge(w_loaded["wq"], 16)
            act.activation(wq_h[:], raw_w[0], ACT.Copy).then_inc(w_hi, 1)
            act.wait_ge(small_loaded, 16 * 9)
            act.activation(tgx[:], gates_in[:, 0:1], ACT.Tanh).then_inc(tanh_done, 1)
            act.activation(tgf[:], gates_in[:, 1:2], ACT.Tanh).then_inc(tanh_done, 1)
            act.wait_ge(kbd_ready, 1)

            def x_hi(w, t):
                act.wait_ge(work_filled, w.count("xT", t))
                act.activation(xnT_h[:, :, t * P:(t + 1) * P],
                               wbank(w.bank("xT", t)).rearrange("p (c n) -> p c n", c=DC), ACT.Copy)\
                    .then_inc(xT_hi, 1)

            def query_hi(w, c):
                act.wait_ge(work_filled, w.count("q", c))
                act.activation(qT_h[:, c, :], wbank(w.bank("q", c)), ACT.Identity,
                               bias=bq_sb[:, c:c + 1]).then_inc(q_hi, 1)

            def exps(g, j, bank):
                if bank == 0:
                    act.wait_ge(nbias_ready, NHALF * g + j + 1)
                    first_wait(act, pT_filled, NHALF * g + j - 1)
                for h in range(HQ * bank, HQ * (bank + 1)):
                    ins = act.activation(prob[:, j % 2, h, :],
                                         psum[:, 2 * (j % 2) + bank, (h % HQ) * KEYS:(h % HQ + 1) * KEYS],
                                         ACT.Exp, bias=nbias[:, j % 2, h:h + 1], scale=SCALE,
                                         accum_out=psums[:, j % 2, h:h + 1])
                if bank == 1:
                    ins.then_inc(exp_done, 1)

            def take_pT(g, j):
                act.wait_ge(pT_filled, NHALF * g + j + 1)
                h0, t = (j // TPG) * HH, j % TPG
                act.activation(probT[:, h0:h0 + HH, t * P:(t + 1) * P],
                               psum[:, 6:8, :].rearrange("p a (h n) -> p (a h) n", h=HQ), ACT.Copy)\
                    .then_inc(pT_taken, 1)

            def use(w, g, kind, i):
                if kind == "xT":
                    x_hi(w, i)
                elif kind == "q":
                    query_hi(w, i)
                elif kind == "pv":
                    act.wait_ge(work_filled, w.count("pv", i))
                    act.activation(oT_h[:, i, :], wbank(w.bank("pv", i)), ACT.Copy).then_inc(o_hi, 1)
                elif kind == "rt":
                    act.wait_ge(vdiff_ready, g - 1)
                    act.activation(gexp[:], vdiff[:], ACT.Exp).then_inc(gexp_done, 1)

            def step(g):
                w = Work(g)
                for j in range(NHALF):
                    first, *others = SLOTS[j]
                    if w.has(first[2]):
                        use(w, g, *first[:2])
                    if j < 2 and w.has(1):
                        take_pT(g - 1, NHALF - 2 + j)
                    if j >= 2 and w.has(0):
                        take_pT(g, j - 2)
                    for kind, i, lag in others:
                        if kind != "q" and w.has(lag):
                            use(w, g, kind, i)
                    if w.has(0):
                        exps(g, j, 0)
                    for kind, i, lag in others:
                        if kind == "q" and w.has(lag):
                            use(w, g, kind, i)
                    if w.has(0):
                        exps(g, j, 1)

            w = Work(-1)
            for t in range(TPG):
                x_hi(w, t)
            for c in range(2):
                query_hi(w, c)
            act.wait_ge(w_loaded["wo"], 16)
            act.activation(wo_h[:], raw_w[3], ACT.Copy).then_inc(w_hi, 1)
            act.wait_ge(init_stored, 16 * (1 + 2 * ST))
            for g in range(LOOP[0]):
                step(g)
            with act.Fori(*LOOP) as g:
                step(g)
            for g in range(LOOP[1], ITERATIONS):
                step(g)
            act.drain().then_inc(phase1_done, 1)
            act.wait_ge(phase1_done, 3)

            def weights_hi(u, e):
                pair, r = (u // UPL) % PAIRS, (u // UPL) % NRAW
                n = u % UPL
                act.wait_ge(raw_loaded[r], e * (32 * PAIRS // NRAW) + 32 * ((u // UPL) // NRAW + 1))
                act.activation(w1_h[:, u % 4], raw1[:, r, n * D:(n + 1) * D].rearrange("p (c n) -> p c n", c=DC),
                               ACT.Copy).then_inc(w1_hi, 1)
                if u >= 4:
                    act.wait_ge(down_done, e * (FU - 1) + u - 3)
                act.activation(w2_h[:, u % 4], raw2[:, r, n * D:(n + 1) * D], ACT.Copy).then_inc(w2_hi, 1)

            def rows_hi(e, i, n):
                act.wait_ge(xg_turned, e * ST + i + 1)
                act.activation(xT_h[:, :, i * P:(i + 1) * P],
                               rows_bank(n, i).rearrange("p (c n) -> p c n", c=DC), ACT.Copy)\
                    .then_inc(xg_hi, 1)

            weights_hi(0, 0)
            weights_hi(1, 0)
            for i in range(ST):
                rows_hi(0, i, None)
            def expert(e, n):
                for u in range(FU):
                    for part, (cols, counts_for) in enumerate(parts_of(n)):
                        act.wait_ge(h_filled, e * (2 * FU) + 2 * u + part + counts_for)
                        hp = h_bank(n, u, part)[:, 0:cols.stop - cols.start]
                        bias = b1_cur[:, u:u + 1]
                        act.activation(h_f[:, u % 3, cols], hp, ACT.Gelu, bias=bias)
                        act.activation(h_h[:, u % 3, cols], hp, ACT.Gelu, bias=bias).then_inc(h_gelu, counts_for)
                    weights_hi(u + 2, e)
                    if u == FU - 2:
                        for i in range(early_rows(n)):
                            rows_hi(e + 1, i, n)
                for i in range(early_rows(n), ST):
                    rows_hi(e + 1, i, n)

            with act.Fori(0, E) as e:
                act.wait_ge(b1_taken, e + 1)
                by_steps(act, e, lambda n: expert(e, n))

        @block.tensor
        def _(pe):
            def product(dst, pairs, cols=None):
                n = len(pairs)
                for i, (ah, al, bh, bl) in enumerate(pairs):
                    pe.matmul(dst, ah, bh, start=(i == 0), stop=False)
                    pe.matmul(dst, ah, bl, start=False, stop=False)
                    ins = pe.matmul(dst, al, bh, start=False, stop=(i == n - 1))
                return ins

            def take(w, use):
                pe.wait_ge(work_drained, w.count(*use) - 2)
                return wbank(w.bank(*use))

            pe.wait_ge(w_loaded["ctx"], 16)
            pe.wait_ge(w_loaded["wk"], 16)
            for c in range(DC):
                if c >= 2:
                    pe.wait_ge(work_drained, c - 1)
                for i in range(DC):
                    ins = pe.matmul(wbank(c % 2)[:, 0:BATCH * KEYS], raw_w[1][:, i, c * P:(c + 1) * P],
                                    ctx_sb[:, i, :], start=(i == 0), stop=(i == DC - 1))
                ins.then_inc(work_filled, 1)
            pe.wait_ge(w_loaded["wv"], 16)
            for b in range(BATCH):
                pe.wait_ge(work_drained, DC + b - 1)
                for i in range(DC):
                    ins = pe.matmul(wbank(b), ctx_sb[:, i, b * KEYS:(b + 1) * KEYS], raw_w[2][:, i, :],
                                    start=(i == 0), stop=(i == DC - 1))
                ins.then_inc(work_filled, 1)
            pe.wait_ge(const_done, 9)

            def turn_x(w, g, t):
                pe.wait_ge(xn_ready, TPG * g + t + 1)
                dst = take(w, ("xT", t))
                for c in range(DC):
                    ins = pe.transpose(dst[:, c * P:(c + 1) * P], xn[:, t % 2, c * P:(c + 1) * P], ident[:])
                ins.then_inc(work_filled, 1)

            def query(w, c):
                if c == 0:
                    pe.wait_ge(work_drained, w.count("xT", TPG - 1))
                dst = take(w, ("q", c))
                cs = slice(c * P, (c + 1) * P)
                product(dst, [(wq_h[:, i, cs], wq_l[:, i, cs], xnT_h[:, i, :], xnT_l[:, i, :])
                              for i in range(DC)]).then_inc(work_filled, 1)

            def scores(w, g, j):
                if j == 0:
                    pe.wait_ge(work_drained, w.count_before("q", 1))
                if j == TPG:
                    pe.wait_ge(work_drained, w.count("q", 3))
                first_wait(pe, exp_done, NHALF * g + j - 1)
                t = j % TPG
                ts = slice(t * P, (t + 1) * P)
                for n in range(2):
                    c = 2 * (j // TPG) + n
                    off = (g // GPB) * (DC * HQ * KEYS) + c * HQ * KEYS
                    kh, kl = (k[:, bass.ds(off, HQ * KEYS)] for k in (kbd_h, kbd_l))
                    ins = product(psum[:, 2 * (j % 2) + n, :], [(qT_h[:, c, ts], qT_l[:, c, ts], kh, kl)])
                ins.then_inc(s_filled, 1)

            def turn_probs(g, j):
                pe.wait_ge(prob_ready, NHALF * g + j + 1)
                first_wait(pe, pT_taken, NHALF * g + j)
                for h in range(HH):
                    ins = pe.transpose(psum[:, 6 + h // HQ, (h % HQ) * P:(h % HQ + 1) * P],
                                       prob[:, j % 2, h, :], ident[:])
                ins.then_inc(pT_filled, 1)

            def context(w, g, c):
                if c % 2 == 0:
                    pe.wait_ge(pT_taken, NHALF * g + TPG * (c // 2 + 1))
                if c == 0:
                    pe.wait_ge(v_ready, g + 1)
                dst = take(w, ("pv", c))
                for n in range(HQ):
                    h = HQ * c + n
                    ins = pe.matmul(dst[n * DH:(n + 1) * DH, :], v_cur[:, h * DH:(h + 1) * DH], probT[:, h, :],
                                    start=True, stop=True)
                ins.then_inc(work_filled, 1)

            def project(w, t):
                if t == 0:
                    pe.wait_ge(work_drained, w.count("pv", DC - 1))
                dst = take(w, ("O", t))
                ts = slice(t * P, (t + 1) * P)
                product(dst, [(oT_h[:, c, ts], oT_l[:, c, ts], wo_h[:, c, :], wo_l[:, c, :])
                              for c in range(DC)]).then_inc(work_filled, 1)

            def turn_x2(w, g, t):
                pe.wait_ge(xn2_ready, TPG * g + t + 1)
                dst = take(w, ("x2T", t))
                for c in range(DC):
                    ins = pe.transpose(dst[:, c * P:(c + 1) * P], xn2[:, t % 2, c * P:(c + 1) * P], ident[:])
                ins.then_inc(work_filled, 1)

            def route_logits(w):
                pe.wait_ge(work_drained, w.count("x2T", TPG - 1))
                dst = take(w, ("lg", 0))
                for t in range(TPG):
                    for c in range(DC):
                        ins = pe.matmul(dst[:, t * E:(t + 1) * E], x2T[:, c, t * P:(t + 1) * P], rw_sb[:, c, :],
                                        start=(c == 0), stop=(c == DC - 1))
                ins.then_inc(work_filled, 1)

            def count_chosen(w, g):
                pe.wait_ge(chosen_ready, g + 1)
                dst = take(w, ("rt", 0))
                m = chosen[:].rearrange("p t e -> p (t e)")
                pe.matmul(dst[:, 0:TPG * E], before[:], m, start=True, stop=True)
                pe.matmul(dst[:, TPG * E:2 * TPG * E], ones[:], m, start=True, stop=True).then_inc(work_filled, 1)

            def use(w, g, kind, i, lag):
                if kind == "O":
                    project(w, i)
                elif kind == "x2T":
                    turn_x2(w, g - lag, i)
                elif kind == "lg":
                    route_logits(w)
                elif kind == "xT":
                    turn_x(w, g + 1, i)
                elif kind == "q":
                    query(w, i)
                elif kind == "pv":
                    context(w, g - lag, i)
                elif kind == "rt":
                    count_chosen(w, g - 2)

            def step(g):
                w = Work(g)
                for j in range(NHALF):
                    first, *others = SLOTS[j]
                    if w.has(first[2]):
                        use(w, g, *first)
                    if j < 2 and w.has(1):
                        turn_probs(g - 1, NHALF - 2 + j)
                    if j >= 2 and w.has(0):
                        turn_probs(g, j - 2)
                    if w.has(0):
                        scores(w, g, j)
                    for other in others:
                        if w.has(other[2]):
                            use(w, g, *other)

            w = Work(-1)
            for t in range(TPG):
                turn_x(w, 0, t)
            pe.wait_ge(wq_split, 1)
            for c in range(2):
                query(w, c)
            pe.wait_ge(kbd_ready, 1)
            pe.wait_ge(wo_split, 1)
            for g in range(LOOP[0]):
                step(g)
            with pe.Fori(*LOOP) as g:
                step(g)
            for g in range(LOOP[1], ITERATIONS):
                step(g)
            pe.drain().then_inc(phase1_done, 1)
            pe.wait_ge(phase1_done, 3)

            def turn_rows(e, tiles, n):
                for i in tiles:
                    pe.wait_ge(gathered[i], 16 * e + 16)
                    if i >= 3:
                        pe.wait_ge(xg_split, e * ST + i - 2)
                    elif n:
                        parts = parts_of(n)
                        turn = len(parts) * FU + i
                        pe.wait_ge(h_split, (e - 1) * (2 * FU) + (turn - 2) * parts[0][1])
                    for c in range(DC):
                        ins = pe.transpose(rows_bank(n, i)[:, c * P:(c + 1) * P], xg[:, i, c * P:(c + 1) * P],
                                           ident[:])
                    ins.then_inc(xg_turned, 1)

            def up(e, u, n):
                pe.wait_ge(w1_split, e * FU + u + 1)
                for part, (cols, counts_for) in enumerate(parts_of(n)):
                    turn = len(parts_of(n)) * u + part
                    if turn < 3:
                        pe.wait_ge(xg_split, (e + 1) * ST)
                    else:
                        pe.wait_ge(h_split, e * (2 * FU) + (turn - 2) * counts_for)
                    ins = product(h_bank(n, u, part)[:, 0:cols.stop - cols.start],
                                  [(w1_h[:, u % 4, c, :], w1_l[:, u % 4, c, :], xT_h[:, c, cols], xT_l[:, c, cols])
                                   for c in range(DC)])
                    ins.then_inc(h_filled, counts_for)

            def down(e, u, n):
                pe.wait_ge(w2_split, e * FU + u + 1)
                pe.wait_ge(h_split, e * (2 * FU) + 2 * u + 2)
                wh, wl = w2_h[:, u % 4, :], w2_l[:, u % 4, :]
                for i, rows, counts_for in tiles_of(n):
                    slots = slice(i * P, i * P + rows)
                    hh, hl = h_h[:, u % 3, slots], h_l[:, u % 3, slots]
                    y = psum[0:rows, i, :]
                    pe.matmul(y, hh, wh, start=(u == 0), stop=False)
                    pe.matmul(y, hh, wl, start=False, stop=False)
                    ins = pe.matmul(y, hl, wh, start=False, stop=(u == FU - 1))
                    if u == FU - 1:
                        ins.then_inc(y_filled, counts_for)
                if u < FU - 1:
                    ins.then_inc(down_done, 1)

            turn_rows(0, range(ST), None)

            def expert(e, n):
                up(e, 0, n)
                up(e, 1, n)
                for u in range(FU):
                    if u == FU - 2:
                        turn_rows(e + 1, range(early_rows(n)), n)
                    if u == FU - 1:
                        turn_rows(e + 1, range(early_rows(n), ST), n)
                    down(e, u, n)
                    if u + 2 < FU:
                        up(e, u + 2, n)

            with pe.Fori(0, E) as e:
                by_steps(pe, e, lambda n: expert(e, n))

        @block.vector
        def _(dve):
            steps = Steps(dve, dve_step)
            link = steps.link

            def f32(ap):
                return ap.bitcast(F32)

            dve.memset(f32(kbd_h[:]), 0.0)
            link(dve.memset(f32(kbd_l[:]), 0.0))
            dve.memset(run[:, 0, :], 0.0)
            dve.wait_ge(const_done, 9)
            dve.tensor_copy(iota_e[:], iota_i[:])
            dve.tensor_copy(tok_f[:], tok_i[:])
            link(dve.tensor_copy(trash_f[:], trash_i[:]))
            assert steps.n == LINKS_PREP, steps.n
            steps.enter(LINKS_PREP)
            for c in range(DC):
                dve.wait_ge(w_hi, c + 1)
                dve.scalar_tensor_tensor(out=xnT_l[:, c, 0:BATCH * KEYS], in0=wbank(c % 2)[:, 0:BATCH * KEYS],
                                         scalar=bk_sb[:, c:c + 1], in1=f32(xnT_h[:, c, 0:BATCH * KEYS]),
                                         op0=ALU.add, op1=ALU.subtract).then_inc(work_drained, 1)

            def take_v():
                dve.wait_ge(small_loaded, 16 * 9)
                for b in range(BATCH):
                    dve.wait_ge(work_filled, DC + b + 1)
                    dve.tensor_tensor(v_all[:, b * D:(b + 1) * D], wbank(b), bv_sb[:], ALU.add)\
                        .then_inc(work_drained, 1)

            def spread_k():
                dve.wait_ge(work_drained, PREP_USES)
                for n in range(HQ):
                    rows = slice(n * DH, (n + 1) * DH)
                    for src, dst in ((xnT_h, kbd_h), (xnT_l, kbd_l)):
                        ins = dve.tensor_copy(
                            dst[rows, :].rearrange("p (b c h k) -> p b c h k", b=BATCH, c=DC, h=HQ)[:, :, :, n, :],
                            f32(src[rows, :, 0:BATCH * KEYS]).rearrange("p c (b k) -> p b c k", b=BATCH))
                ins.then_inc(kbd_ready, 1)
                dve.wait_ge(kbd_ready, 1)

            def row_stats(src, t):
                steps.mark(dve.bn_stats(stats[:, t, :], src))

            def row_means(to, a, b):
                steps.wait()
                dve.sem_inc(passed, 1)
                for t in range(a, b):
                    ins = dve.bn_aggr(to[0][:, t, :], stats[:, t, :])
                steps.mark(ins)

            def root_seed(to, a, b):
                mv, rs = to
                steps.wait()
                link(dve.tensor_scalar(ve[:, a:b], mv[:, a:b, 1], EPS, None, ALU.add))
                dve.tensor_scalar(nhv[:, a:b], ve[:, a:b], -0.5, None, ALU.mult)
                link(dve.tensor_scalar(nt[:, a:b].bitcast(I32), ve[:, a:b].bitcast(I32), 1, None,
                                       ALU.logical_shift_right))
                steps.mark(dve.tensor_scalar(rs[:, a:b].bitcast(I32), nt[:, a:b].bitcast(I32), -1.0,
                                               1597463007.0, ALU.mult, ALU.add))

            def root_round(to, a, b):
                rs = to[1]
                steps.wait()
                link(dve.tensor_tensor(nt[:, a:b], rs[:, a:b], rs[:, a:b], ALU.mult))
                link(dve.tensor_tensor(nt[:, a:b], nt[:, a:b], nhv[:, a:b], ALU.mult))
                steps.mark(dve.scalar_tensor_tensor(out=rs[:, a:b], in0=nt[:, a:b], scalar=1.5,
                                                      in1=rs[:, a:b], op0=ALU.add, op1=ALU.mult))

            def normalise(dst, src, t, to):
                mv, rs = to
                steps.wait()
                return dve.tensor_scalar(dst, src, mv[:, t, 0:1], rs[:, t:t + 1], ALU.subtract, ALU.mult)

            def x_stats(g, t):
                if t == 0:
                    dve.wait_ge(x_loaded, 16 * g + 16)
                row_stats(x_sb[:, t, :], t)

            def x_norm(t):
                normalise(xn[:, t % 2, :], x_sb[:, t, :], t, x_mv).then_inc(xn_ready, 1)

            def x_lo(w, g, t):
                dve.wait_ge(xT_hi, TPG * g + t + 1)
                ts = slice(t * P, (t + 1) * P)
                dve.tensor_tensor(xnT_l[:, :, ts], wbank(w.bank("xT", t)).rearrange("p (c n) -> p c n", c=DC),
                                  f32(xnT_h[:, :, ts]), ALU.subtract).then_inc(work_drained, 1)

            def query_lo(w, g, c):
                dve.wait_ge(q_hi, DC * g + c + 1)
                dve.scalar_tensor_tensor(out=qT_l[:, c, :], in0=wbank(w.bank("q", c)),
                                         scalar=bq_sb[:, c:c + 1], in1=f32(qT_h[:, c, :]),
                                         op0=ALU.add, op1=ALU.subtract).then_inc(work_drained, 1)

            def context_lo(w, g, c):
                dve.wait_ge(o_hi, DC * g + c + 1)
                dve.tensor_tensor(oT_l[:, c, :], wbank(w.bank("pv", c)), f32(oT_h[:, c, :]),
                                  ALU.subtract).then_inc(work_drained, 1)

            def row_max(g, j):
                b = j % 2
                dve.wait_ge(s_filled, NHALF * g + j + 1)
                steps.mark(dve.tensor_reduce(
                    nmax[:, b, :].rearrange("p (a h) -> p a h", a=2),
                    psum[:, 2 * b:2 * b + 2, :].rearrange("p a (h k) -> p a h k", h=HQ),
                    AX.X, ALU.max, negate=True))
                return steps.base + steps.n

            def scale_max(j, found):
                b = j % 2
                dve.wait_ge(dve_step, found)
                dve.tensor_scalar(nbias[:, b, :], nmax[:, b, :], SCALE, None, ALU.mult).then_inc(nbias_ready, 1)

            def reciprocals(g, j):
                b = j % 2
                dve.wait_ge(exp_done, NHALF * g + j + 1)
                dve.reciprocal(rinv[:, b, :], psums[:, b, :]).then_inc(rinv_ready, 1)

            def residual(w, g, t):
                if t == 0:
                    dve.wait_ge(xr_ready, g + 1)
                if t == 0:
                    first_wait(dve, xn2_ready, g * TPG)
                    first_wait(dve, x2_stored[0], g * (16 * 2))
                    first_wait(dve, x2_stored[1], g * (16 * 2))
                if t == 3:
                    dve.wait_ge(xn2_ready, g * TPG + 1)
                    dve.wait_ge(x2_stored[0], g * (16 * 2) + 16)
                dve.wait_ge(work_filled, w.count("O", t))
                dve.scalar_tensor_tensor(out=x2[:, t % 3, :], in0=wbank(w.bank("O", t)), scalar=tgx[:, 0:1],
                                         in1=xr[:, t, :], op0=ALU.mult, op1=ALU.add).then_inc(work_drained, 1)

            def x2_stats(w, t):
                dve.wait_ge(work_drained, w.count("O", t))
                row_stats(x2[:, t % 3, :], t)

            def x2_norm(g, t):
                first_wait(dve, xn2_stored[t % 2], g * (16 * TPG // 2) + 16 * (t // 2))
                normalise(xn2[:, t % 2, :], x2[:, t % 3, :], t, pair_mv).then_inc(xn2_ready, 1)

            def take_x2T(w, t):
                dve.wait_ge(work_filled, w.count("x2T", t))
                dve.tensor_copy(x2T[:, :, t * P:(t + 1) * P],
                                wbank(w.bank("x2T", t)).rearrange("p (c n) -> p c n", c=DC))\
                    .then_inc(work_drained, 1)

            def take_logits(w):
                dve.wait_ge(work_filled, w.count("lg", 0))
                dve.tensor_tensor(logits[:], wbank(w.bank("lg", 0))[:, 0:TPG * E].rearrange(
                    "p (t e) -> p t e", t=TPG), rb_sb[:, None, :].broadcast_to([P, TPG, E]), ALU.add)\
                    .then_inc(work_drained, 1)

            def take_counts(w):
                dve.wait_ge(work_filled, w.count("rt", 0))
                dve.tensor_copy(counts[:].rearrange("p a t e -> p (a t e)"),
                                wbank(w.bank("rt", 0))[:, 0:2 * TPG * E]).then_inc(work_drained, 1)

            def choose(w, part):
                if part == 0:
                    wait_apart(dve, work_drained, w.count("lg", 0))
                    for t in range(TPG):
                        ins = dve.max(top[:, t, :], logits[:, t, :])
                    steps.mark(ins)
                elif part == 1:
                    steps.wait()
                    dve.sem_inc(passed, 1)
                    for t in range(TPG):
                        ins = dve.max_index(topi[:, t, :], top[:, t, :], logits[:, t, :])
                    steps.mark(ins)
                else:
                    steps.wait()
                    dve.tensor_tensor(vdiff[:], top[:, :, 1], top[:, :, 0], ALU.subtract).then_inc(vdiff_ready, 1)
                    link(dve.tensor_copy(topf[:], topi[:, :, 0:2].rearrange("p t k -> p k t")))
                    for k in range(2):
                        ins = dve.tensor_tensor(onehot[:, k], iota_e[:, None, :].broadcast_to([P, TPG, E]),
                                                topf[:, k, :, None].broadcast_to([P, TPG, E]), ALU.is_equal)
                    link(ins)
                    dve.tensor_tensor(chosen[:], onehot[:, 0], onehot[:, 1], ALU.add).then_inc(chosen_ready, 1)

            def place(w, g, part):
                if part == 0:
                    dve.wait_ge(work_drained, w.count("rt", 0))
                    for t in range(TPG):
                        link(dve.tensor_tensor(run[:, t + 1, :], run[:, t, :], counts[:, 1, t, :], ALU.add))
                    steps.mark(dve.tensor_tensor(pos[:], counts[:, 0], run[:, 0:TPG, :], ALU.add))
                elif part == 1:
                    steps.wait()
                    dve.tensor_copy(run[:, 0, :], run[:, TPG, :])
                    for k in range(2):
                        ins = dve.tensor_tensor(prod[:, k], onehot[:, k], pos[:], ALU.mult)
                    link(ins)
                    link(dve.tensor_reduce(pk[:], prod[:], AX.X, ALU.add))
                    dve.tensor_scalar(kept[:], pk[:], float(CAP), None, ALU.is_lt)
                    steps.mark(dve.tensor_scalar(offs[:], pk[:], float(P), None, ALU.is_ge))
                elif part == 2:
                    steps.wait()
                    for m in range(2, ST):
                        link(dve.scalar_tensor_tensor(out=offs[:], in0=pk[:], scalar=float(m * P), in1=offs[:],
                                                      op0=ALU.is_ge, op1=ALU.add))
                    link(dve.tensor_scalar(offs[:], offs[:], -float(P * ST - 1), None, ALU.mult))
                    link(dve.scalar_tensor_tensor(out=dest_f[:], in0=pk[:], scalar=float(ST), in1=offs[:],
                                                  op0=ALU.mult, op1=ALU.add))
                    steps.mark(dve.scalar_tensor_tensor(out=dest_f[:], in0=topf[:], scalar=float(CAP),
                                                          in1=dest_f[:], op0=ALU.mult, op1=ALU.add))
                elif part == 3:
                    steps.wait()
                    dve.wait_ge(gexp_done, g + 1)
                    link(dve.tensor_scalar(den[:], gexp[:], 1.0, None, ALU.add))
                    dve.tensor_tensor(dest_f[:], dest_f[:], trash_f[:], ALU.subtract)
                    link(dve.reciprocal(gk[:, 0, :], den[:]))
                    dve.tensor_tensor(dest_f[:], dest_f[:], kept[:], ALU.mult)
                    link(dve.tensor_tensor(gk[:, 1, :], gk[:, 0, :], gexp[:], ALU.mult))
                    dve.tensor_tensor(dest_f[:], dest_f[:], trash_f[:], ALU.add)
                    link(dve.tensor_tensor(gk[:], gk[:], kept[:], ALU.mult))
                    steps.mark(dve.tensor_tensor(den[:], gk[:, 0, :], gk[:, 1, :], ALU.add))
                else:
                    steps.wait()
                    link(dve.tensor_scalar(den[:], den[:], 1e-9, None, ALU.add))
                    link(dve.reciprocal(den[:], den[:]))
                    for k in range(2):
                        ins = dve.tensor_tensor(gk[:, k, :], gk[:, k, :], den[:], ALU.mult)
                    link(ins)
                    dve.wait_ge(entry_free, g + 1)
                    dve.tensor_copy(dest[:], dest_f[:])
                    for k in range(2):
                        dve.tensor_copy(entry[:, k, :, 0], tok_f[:])
                    link(dve.tensor_scalar(entry[:, :, :, 1].bitcast(F32), gk[:], tgf[:, 0:1], None, ALU.mult))
                    dve.tensor_scalar(tok_f[:], tok_f[:], float(GT), None, ALU.add)
                    dve.tensor_scalar(trash_f[:], trash_f[:], float(GT), None, ALU.add).then_inc(entry_ready, 1)

            def piece(w, g, name):
                what, *rest = name.split()
                i = int(rest[-1]) if rest and rest[-1].isdigit() else None
                lag = SIDE_LAG[what]
                if not w.has(lag):
                    return
                if what == "v":
                    dve.tensor_scalar(v_cur[:], v_all[:, bass.ds((g // GPB) * D, D)], 1.0, None, ALU.mult)\
                        .then_inc(v_ready, 1)
                elif what == "c":
                    choose(w, i)
                elif what == "t":
                    place(w, g - lag, i)
                else:
                    to, a, b = {"x": (x_mv, 0, TPG), "p": (pair_mv, 0, 2)}.get(what, (pair_mv, 2, 4))
                    if rest[0] == "stats":
                        x_stats(g - lag, i) if what == "x" else x2_stats(w, i)
                    elif rest[0] == "mean":
                        row_means(to, a, b)
                    elif rest[0] == "seed":
                        root_seed(to, a, b)
                    elif rest[0] == "root":
                        root_round(to, a, b)
                    else:
                        x_norm(i) if what == "x" else x2_norm(g - lag, i)

            def drain(w, g, kind, i, lag):
                if kind == "O":
                    residual(w, g - 1, i)
                elif kind == "x2T":
                    take_x2T(w, i)
                elif kind == "lg":
                    take_logits(w)
                elif kind == "xT":
                    x_lo(w, g + 1, i)
                elif kind == "q":
                    query_lo(w, g - lag, i)
                elif kind == "pv":
                    context_lo(w, g - lag, i)
                elif kind == "rt":
                    take_counts(w)

            def step(g, links):
                steps.enter(links)
                w = Work(g)
                for j in range(NHALF):
                    after_first, after_max, after_scaling, *after_others = SIDE[j]
                    first, *others = SLOTS[j]
                    if w.has(first[2]):
                        drain(w, g, *first)
                    for name in after_first:
                        piece(w, g, name)
                    if j >= 1 and w.has(0):
                        reciprocals(g, j - 1)
                    if j == 0 and w.has(1):
                        reciprocals(g - 1, NHALF - 1)
                    if w.has(0):
                        found = row_max(g, j)
                    for name in after_max:
                        piece(w, g, name)
                    if w.has(0):
                        scale_max(j, found)
                    for name in after_scaling:
                        piece(w, g, name)
                    for other, pieces in zip(others, after_others):
                        if w.has(other[2]):
                            drain(w, g, *other)
                        for name in pieces:
                            piece(w, g, name)
                assert steps.n == links_of(g), (steps.n, links_of(g))

            w = Work(-1)
            for t in range(TPG):
                x_stats(0, t)
            row_means(x_mv, 0, TPG)
            root_seed(x_mv, 0, TPG)
            for _ in range(3):
                root_round(x_mv, 0, TPG)
            for t in range(2):
                x_norm(t)
            take_v()
            spread_k()
            for t in range(TPG):
                x_lo(w, 0, t)
                if t + 2 < TPG:
                    x_norm(t + 2)
                if t == 0:
                    dve.wait_ge(w_hi, DC + 1)
                    dve.tensor_tensor(wq_l[:], raw_w[0], f32(wq_h[:]), ALU.subtract).then_inc(wq_split, 1)
            dve.wait_ge(tanh_done, 2)
            dve.tensor_scalar(bo_sb[:], bo_sb[:], tgx[:, 0:1], None, ALU.mult).then_inc(bo_ready, 1)
            for c in range(2):
                query_lo(w, 0, c)
            dve.wait_ge(w_hi, DC + 2)
            dve.tensor_tensor(wo_l[:], raw_w[3], f32(wo_h[:]), ALU.subtract).then_inc(wo_split, 1)
            base = LINKS_PREP + links_of(-1)
            for g in range(LOOP[0]):
                step(g, base)
                base += links_of(g)
            with dve.Fori(*LOOP) as g:
                step(g, (g - LOOP[0]) * links_of(g) + base)
            base += links_of(LOOP[0]) * (LOOP[1] - LOOP[0])
            for g in range(LOOP[1], ITERATIONS):
                step(g, base)
                base += links_of(g)
            steps.enter(base)
            steps.wait()
            link(dve.tensor_scalar(pos[:, 0, :], run[:, 0, :], float(LEAST * STEP), None, ALU.is_gt))
            for m in range(LEAST + 1, STEPS):
                link(dve.scalar_tensor_tensor(out=pos[:, 0, :], in0=run[:, 0, :], scalar=float(m * STEP),
                                              in1=pos[:, 0, :], op0=ALU.is_gt, op1=ALU.add))
            dve.tensor_scalar(n_steps[:], pos[:, 0, :], float(LEAST), None, ALU.add)
            dve.drain().then_inc(phase1_done, 1)
            dve.wait_ge(phase1_done, 3)

            def weights_lo(u, e):
                r, n, k = (u // UPL) % NRAW, u % UPL, e * FU + u + 1
                dve.wait_ge(w1_hi, k)
                dve.tensor_tensor(w1_l[:, u % 4], raw1[:, r, n * D:(n + 1) * D].rearrange("p (c n) -> p c n", c=DC),
                                  f32(w1_h[:, u % 4]), ALU.subtract).then_inc(w1_split, 1)
                dve.wait_ge(w2_hi, k)
                dve.tensor_tensor(w2_l[:, u % 4], raw2[:, r, n * D:(n + 1) * D], f32(w2_h[:, u % 4]),
                                  ALU.subtract).then_inc(w2_split, 1)

            def rows_lo(e, i, n):
                dve.wait_ge(xg_hi, e * ST + i + 1)
                cols = slice(i * P, (i + 1) * P)
                dve.tensor_tensor(xT_l[:, :, cols], rows_bank(n, i).rearrange("p (c n) -> p c n", c=DC),
                                  f32(xT_h[:, :, cols]), ALU.subtract).then_inc(xg_split, 1)

            def take_b1(e):
                dve.tensor_scalar(b1_cur[:], b1_sb[:, bass.ds(e * FU, FU)], 1.0, None, ALU.mult)\
                    .then_inc(b1_taken, 1)

            take_b1(0)
            weights_lo(0, 0)
            weights_lo(1, 0)
            for i in range(ST):
                rows_lo(0, i, None)

            def expert(e, n):
                for u in range(FU):
                    for part, (cols, counts_for) in enumerate(parts_of(n)):
                        dve.wait_ge(h_gelu, e * (2 * FU) + 2 * u + part + counts_for)
                        dve.tensor_tensor(h_l[:, u % 3, cols], h_f[:, u % 3, cols], f32(h_h[:, u % 3, cols]),
                                          ALU.subtract).then_inc(h_split, counts_for)
                    if u == FU - 1:
                        take_b1(e + 1)
                    weights_lo(u + 2, e)
                    if u == FU - 2:
                        for i in range(early_rows(n)):
                            rows_lo(e + 1, i, n)
                for i in range(early_rows(n), ST):
                    rows_lo(e + 1, i, n)
                dve.wait_ge(b2_loaded, 16 * e + 16)
                dve.wait_ge(y_free, e + 1)
                for i, rows, counts_for in tiles_of(n):
                    dve.wait_ge(y_filled, e * ST + i + 1)
                    dve.tensor_tensor(y_sb[0:rows, i, :], psum[0:rows, i, :], b2_sb[0:rows, :], ALU.add)\
                        .then_inc(y_biased, counts_for)

            with dve.Fori(0, E) as e:
                by_steps(dve, e, lambda n: expert(e, n))


def _cols(v):
    import numpy as np
    return np.ascontiguousarray(v.reshape(-1, P).T)


def kernel(x, ctx_1024, g_xattn, g_ffn, L0_xattn_w_q, L0_xattn_b_q, L0_xattn_w_k, L0_xattn_b_k, L0_xattn_w_v,
           L0_xattn_b_v, L0_xattn_w_o, L0_xattn_b_o, L0_ffn_router_w, L0_ffn_router_b, L0_ffn_w1, L0_ffn_b1,
           L0_ffn_w2, L0_ffn_b2):
    import numpy as np
    import concourse.bacc as bacc
    from concourse.bass_utils import run_bass_kernel_spmd

    def t(a):
        return np.ascontiguousarray(np.asarray(a).T)

    w1 = np.asarray(L0_ffn_w1).reshape(E, DC, P, PAIRS, UPL, P).transpose(0, 3, 2, 4, 1, 5)
    w2 = np.asarray(L0_ffn_w2).reshape(E, PAIRS, UPL, P, D).transpose(0, 1, 3, 2, 4)
    ins = [
        ("x", np.asarray(x).reshape(TOK, D)),
        ("ctxT", t(np.asarray(ctx_1024).reshape(BATCH * KEYS, D))),
        ("gx", np.asarray(g_xattn).reshape(1, 1)),
        ("gf", np.asarray(g_ffn).reshape(1, 1)),
        ("wqT", t(L0_xattn_w_q)), ("bq", _cols(np.asarray(L0_xattn_b_q))),
        ("wkT", t(L0_xattn_w_k)), ("bk", _cols(np.asarray(L0_xattn_b_k))),
        ("wvT", t(L0_xattn_w_v)), ("bv", np.asarray(L0_xattn_b_v).reshape(1, D)),
        ("woT", t(L0_xattn_w_o)), ("bo", np.asarray(L0_xattn_b_o).reshape(1, D)),
        ("rwT", t(L0_ffn_router_w)), ("rb", np.asarray(L0_ffn_router_b).reshape(1, E)),
        ("w1", np.ascontiguousarray(w1).reshape(E * PAIRS, P, UPL * D)),
        ("b1", _cols(np.asarray(L0_ffn_b1))),
        ("w2", np.ascontiguousarray(w2).reshape(E * PAIRS, P, UPL * D)),
        ("b2", np.asarray(L0_ffn_b2)),
    ]
    nc = bacc.Bacc("TRN2", target_bir_lowering=False, num_devices=1)
    arrays, args = {}, []
    for name, a in ins:
        a = np.ascontiguousarray(a)
        arrays["in_" + name] = a
        args.append(nc.dram_tensor("in_" + name, a.shape, mybir.dt.from_np(a.dtype), kind="ExternalInput").ap())
    args.append(nc.dram_tensor("out_rows", [TOK + CAP, D], F32, kind="ExternalOutput").ap())
    build(nc, *args)
    r = run_bass_kernel_spmd(nc, [arrays], core_ids=[0])
    return r.results[0]["out_rows"][:TOK].reshape(BATCH, SEQ, D)
```
